# Optimizing a Trainium2 kernel written in Bass

```python
import numpy as np
import jax
import jax.numpy as jnp

def _softmax(x, axis=-1):
    return jax.nn.softmax(x, axis=axis)

def _gelu(x):
    return jax.nn.gelu(x, approximate=True)

def _silu(x):
    return jax.nn.silu(x)

def _sigmoid(x):
    return jax.nn.sigmoid(x)

def _layernorm(x, axis=-1, eps=1e-05):
    m = jnp.mean(x, axis=axis, keepdims=True)
    v = jnp.var(x, axis=axis, keepdims=True)
    return (x - m) / jnp.sqrt(v + eps)

def _scatter_add(tgt, idx, src, axis=0):
    return tgt.at[idx].add(src)

def _segment_sum(src, seg, n):
    return jax.ops.segment_sum(src, seg, n)
kernel_name = 'mk_adj_preln_d4_adj_r2_8af697'

def setup_inputs(seed: int=0):
    np.random.seed(seed)
    _w = jnp.asarray

    def _rec_inputs():
        import jax
        import jax.numpy as jnp
        _gk = jax.random.key(seed)
        x = -0.0001538 + 1 * jax.random.normal(jax.random.fold_in(_gk, 1), (128, 64, 384), jnp.float32)
        _w = (1.0 + jnp.arange(64, dtype=jnp.float32)) ** (-0.5)
        _w = _w / _w.mean()
        _pij = jnp.clip(0.0625 * _w[:, None] * _w[None, :], 0.0, 1.0)
        _a = jax.random.uniform(jax.random.fold_in(_gk, 2), (128, 64, 64)) < _pij
        _a = jnp.logical_or(_a, jnp.swapaxes(_a, -1, -2))
        _a = jnp.logical_or(_a, jnp.eye(64, dtype=bool))
        _af = _a.astype(jnp.float32)
        _af = _af * jax.random.uniform(jax.random.fold_in(_gk, 3), (128, 64, 64), jnp.float32, 0.05, 4.42607)
        adj = _af
        return (x, adj)
    x, adj = _rec_inputs()

    def _L0_gnn_setup():
        import jax, jax.numpy as jnp
        import numpy as np
        NUM_HEADS = 12
        HIDDEN = 384
        HEAD = HIDDEN // NUM_HEADS
        SCALE = HIDDEN ** (-0.5)
        key = jax.random.key(seed)
        ks = jax.random.split(key, 8)
        B, N = (16, 256)
        std = HIDDEN ** (-0.5)
        return {'x': jax.random.normal(ks[0], (B, N, HIDDEN), dtype=jnp.float32), 'encoding_bias': jax.random.normal(ks[1], (B, N, N), dtype=jnp.float32), 'Wq': jax.random.normal(ks[2], (HIDDEN, HIDDEN), dtype=jnp.float32) * std, 'Wk': jax.random.normal(ks[3], (HIDDEN, HIDDEN), dtype=jnp.float32) * std, 'Wv': jax.random.normal(ks[4], (HIDDEN, HIDDEN), dtype=jnp.float32) * std, 'bv': jax.random.normal(ks[5], (HIDDEN,), dtype=jnp.float32) * 0.01, 'Wo': jax.random.normal(ks[6], (HIDDEN, HIDDEN), dtype=jnp.float32) * std, 'bo': jax.random.normal(ks[7], (HIDDEN,), dtype=jnp.float32) * 0.01}
    _L0_gnn_all = _L0_gnn_setup()
    _L0_gnn_in = {k: v for k, v in _L0_gnn_all.items() if k in ('Wq', 'Wk', 'Wv', 'bv', 'Wo', 'bo')}
    del _L0_gnn_all

    def _L1_gnn_setup():
        import jax, jax.numpy as jnp
        import numpy as np
        B, S, H, L = (32, 256, 384, 2)

        def _layer_norm(z, a, b, eps=0.001):
            mu = jnp.mean(z, axis=-1, keepdims=True)
            sigma = jnp.std(z, axis=-1, keepdims=True, ddof=1)
            return (z - mu) / (sigma + eps) * a + b
        key = jax.random.key(seed)
        ks = jax.random.split(key, 6)
        hidden_state = jax.random.normal(ks[0], (B, S, H), dtype=jnp.float32)
        adjacency_matrix = (jax.random.uniform(ks[1], (B, S, S)) < 0.2).astype(jnp.float32)
        W_left = 0.05 * jax.random.normal(ks[2], (L, H, H), dtype=jnp.float32)
        W_right = 0.05 * jax.random.normal(ks[3], (L, H, H), dtype=jnp.float32)
        W_lin = 0.05 * jax.random.normal(ks[4], (L, H, H), dtype=jnp.float32)
        b_lin = jnp.zeros((L, H), dtype=jnp.float32)
        ln_a = jnp.ones((L, H), dtype=jnp.float32)
        ln_b = jnp.zeros((L, H), dtype=jnp.float32)
        return {'hidden_state': hidden_state, 'adjacency_matrix': adjacency_matrix, 'W_left': W_left, 'W_right': W_right, 'W_lin': W_lin, 'b_lin': b_lin, 'ln_a': ln_a, 'ln_b': ln_b}
    _L1_gnn_all = _L1_gnn_setup()
    _L1_gnn_in = {k: v for k, v in _L1_gnn_all.items() if k in ('W_left', 'W_right', 'W_lin', 'b_lin', 'ln_a', 'ln_b')}
    del _L1_gnn_all

    def _L2_gnn_setup():
        import jax, jax.numpy as jnp
        import numpy as np
        LN_EPS = 1e-12

        def _digcn_forward(hidden_state, adjacency_matrix, Wl, bl, Ws, bs, Wr, br, ln_w, ln_b):
            B, S, D = hidden_state.shape
            temper = jnp.asarray(D, jnp.float32) ** 0.5
            i = jnp.arange(S)
            upper = (i[None, :] > i[:, None]).astype(hidden_state.dtype)
            lower = (i[None, :] < i[:, None]).astype(hidden_state.dtype)

            def layer(h, params):
                wl, b_l, ws, b_s, wr, b_r, g, beta = params
                u = jnp.einsum('bid,bjd->bij', h, h) / temper
                a = jax.nn.softmax(u, axis=-1)
                delta = a * adjacency_matrix
                attn = delta / (jnp.sum(delta, axis=-1, keepdims=True) + 1e-10)
                hl = h @ wl.T + b_l
                hs = h @ ws.T + b_s
                hr = h @ wr.T + b_r
                diag_a = jnp.diagonal(attn, axis1=1, axis2=2)
                ctx = jnp.einsum('bij,bjd->bid', attn * upper, hl) + diag_a[..., None] * hs + jnp.einsum('bij,bjd->bid', attn * lower, hr)
                mean = ctx.mean(-1, keepdims=True)
                var = ctx.var(-1, keepdims=True)
                o = (ctx - mean) / jnp.sqrt(var + LN_EPS) * g + beta
                return (jax.nn.relu(o), None)
            out, _ = jax.lax.scan(layer, hidden_state, (Wl, bl, Ws, bs, Wr, br, ln_w, ln_b))
            return out
        key = jax.random.key(seed)
        ks = jax.random.split(key, 6)
        B, S, D, L = (8, 512, 384, 2)
        scale = (1.0 / D) ** 0.5
        hidden_state = jax.random.normal(ks[0], (B, S, D), jnp.float32)
        adjacency_matrix = (jax.random.uniform(ks[1], (B, S, S)) < 0.05).astype(jnp.float32)
        Wl = jax.random.normal(ks[2], (L, D, D), jnp.float32) * scale
        Ws = jax.random.normal(ks[3], (L, D, D), jnp.float32) * scale
        Wr = jax.random.normal(ks[4], (L, D, D), jnp.float32) * scale
        bl = jnp.zeros((L, D), jnp.float32)
        bs = jnp.zeros((L, D), jnp.float32)
        br = jnp.zeros((L, D), jnp.float32)
        ln_w = jnp.ones((L, D), jnp.float32)
        ln_b = jnp.zeros((L, D), jnp.float32)
        return dict(hidden_state=hidden_state, adjacency_matrix=adjacency_matrix, Wl=Wl, bl=bl, Ws=Ws, bs=bs, Wr=Wr, br=br, ln_w=ln_w, ln_b=ln_b)
    _L2_gnn_all = _L2_gnn_setup()
    _L2_gnn_in = {k: v for k, v in _L2_gnn_all.items() if k in ('Wl', 'bl', 'Ws', 'bs', 'Wr', 'br', 'ln_w', 'ln_b')}
    del _L2_gnn_all

    def _L3_gnn_setup():
        import jax, jax.numpy as jnp
        import numpy as np
        B, N, D, H = (8, 512, 384, 12)
        HD = D // H

        def _split_heads(x):
            b, n, _ = x.shape
            return x.reshape(b, n, H, HD).transpose(0, 2, 1, 3)
        key = jax.random.key(seed)
        ks = jax.random.split(key, 10)
        input_graph = jax.random.normal(ks[0], (B, N, D), dtype=jnp.float32)
        u = jax.random.uniform(ks[1], (B, N, N), dtype=jnp.float32)
        keep = jax.random.uniform(ks[2], (B, N, N)) < 0.15
        adj = jnp.where(keep, u, 0.0)
        s = 1.0 / np.sqrt(D)
        Wq = jax.random.normal(ks[3], (D, D), dtype=jnp.float32) * s
        bq = jnp.zeros((D,), dtype=jnp.float32)
        Wk = jax.random.normal(ks[4], (D, D), dtype=jnp.float32) * s
        bk = jnp.zeros((D,), dtype=jnp.float32)
        Wv = jax.random.normal(ks[5], (D, D), dtype=jnp.float32) * s
        bv = jnp.zeros((D,), dtype=jnp.float32)
        beta = jnp.asarray(0.1, dtype=jnp.float32)
        return {'input_graph': input_graph, 'adj': adj, 'Wq': Wq, 'bq': bq, 'Wk': Wk, 'bk': bk, 'Wv': Wv, 'bv': bv, 'beta': beta}
    _L3_gnn_all = _L3_gnn_setup()
    _L3_gnn_in = {k: v for k, v in _L3_gnn_all.items() if k in ('Wq', 'bq', 'Wk', 'bk', 'Wv', 'bv', 'beta')}
    del _L3_gnn_all
    return {'x': x, 'adj': adj, 'L0_gnn_Wq': _L0_gnn_in['Wq'], 'L0_gnn_Wk': _L0_gnn_in['Wk'], 'L0_gnn_Wv': _L0_gnn_in['Wv'], 'L0_gnn_bv': _L0_gnn_in['bv'], 'L0_gnn_Wo': _L0_gnn_in['Wo'], 'L0_gnn_bo': _L0_gnn_in['bo'], 'L1_gnn_W_left': _L1_gnn_in['W_left'], 'L1_gnn_W_right': _L1_gnn_in['W_right'], 'L1_gnn_W_lin': _L1_gnn_in['W_lin'], 'L1_gnn_b_lin': _L1_gnn_in['b_lin'], 'L1_gnn_ln_a': _L1_gnn_in['ln_a'], 'L1_gnn_ln_b': _L1_gnn_in['ln_b'], 'L2_gnn_Wl': _L2_gnn_in['Wl'], 'L2_gnn_bl': _L2_gnn_in['bl'], 'L2_gnn_Ws': _L2_gnn_in['Ws'], 'L2_gnn_bs': _L2_gnn_in['bs'], 'L2_gnn_Wr': _L2_gnn_in['Wr'], 'L2_gnn_br': _L2_gnn_in['br'], 'L2_gnn_ln_w': _L2_gnn_in['ln_w'], 'L2_gnn_ln_b': _L2_gnn_in['ln_b'], 'L3_gnn_Wq': _L3_gnn_in['Wq'], 'L3_gnn_bq': _L3_gnn_in['bq'], 'L3_gnn_Wk': _L3_gnn_in['Wk'], 'L3_gnn_bk': _L3_gnn_in['bk'], 'L3_gnn_Wv': _L3_gnn_in['Wv'], 'L3_gnn_bv': _L3_gnn_in['bv'], 'L3_gnn_beta': _L3_gnn_in['beta']}

def reference(x, adj, L0_gnn_Wq, L0_gnn_Wk, L0_gnn_Wv, L0_gnn_bv, L0_gnn_Wo, L0_gnn_bo, L1_gnn_W_left, L1_gnn_W_right, L1_gnn_W_lin, L1_gnn_b_lin, L1_gnn_ln_a, L1_gnn_ln_b, L2_gnn_Wl, L2_gnn_bl, L2_gnn_Ws, L2_gnn_bs, L2_gnn_Wr, L2_gnn_br, L2_gnn_ln_w, L2_gnn_ln_b, L3_gnn_Wq, L3_gnn_bq, L3_gnn_Wk, L3_gnn_bk, L3_gnn_Wv, L3_gnn_bv, L3_gnn_beta):
    import jax
    import jax.numpy as jnp

    def _L0_gnn_ref(x, encoding_bias, Wq, Wk, Wv, bv, Wo, bo):
        import jax, jax.numpy as jnp
        import numpy as np
        NUM_HEADS = 12
        HIDDEN = 384
        HEAD = HIDDEN // NUM_HEADS
        SCALE = HIDDEN ** (-0.5)
        B, N, _ = x.shape
        q = (x @ Wq.T).reshape(B, N, NUM_HEADS, HEAD)
        k = (x @ Wk.T).reshape(B, N, NUM_HEADS, HEAD)
        v = (x @ Wv.T + bv).reshape(B, N, NUM_HEADS, HEAD)
        a = jnp.einsum('bnhd,bmhd->bhnm', q, k) * SCALE + encoding_bias[:, None, :, :]
        pad_mask = jnp.all(a == 0, axis=-1)
        a = jnp.where(pad_mask[..., None], -jnp.inf, a)
        a = jax.nn.softmax(a, axis=-1)
        a = jnp.nan_to_num(a)
        o = jnp.einsum('bhnm,bmhd->bnhd', a, v).reshape(B, N, HIDDEN)
        return o @ Wo.T + bo

    def _L1_gnn_ref(hidden_state, adjacency_matrix, W_left, W_right, W_lin, b_lin, ln_a, ln_b):
        import jax, jax.numpy as jnp
        import numpy as np
        B, S, H, L = (32, 256, 384, 2)

        def _layer_norm(z, a, b, eps=0.001):
            mu = jnp.mean(z, axis=-1, keepdims=True)
            sigma = jnp.std(z, axis=-1, keepdims=True, ddof=1)
            return (z - mu) / (sigma + eps) * a + b
        temper = float(np.sqrt(H))
        adj = adjacency_matrix
        adj_tri = jnp.triu(adj, k=1)
        diag_mask = jnp.triu(adj, k=0) - adj_tri
        h = hidden_state
        for l in range(L):
            m_left = jnp.einsum('bsh,oh->bso', h, W_left[l])
            m_right = jnp.einsum('bsh,oh->bso', h, W_right[l])
            u_left = jnp.einsum('bih,bjh->bij', h, m_left) / temper
            u_right = jnp.einsum('bih,bjh->bij', h, m_right) / temper
            u = u_left * adj_tri + u_left * diag_mask + u_right * jnp.swapaxes(adj_tri, 1, 2)
            delta_exp_u = jnp.exp(u) * adj
            attention = delta_exp_u / (jnp.sum(delta_exp_u, axis=2, keepdims=True) + 1e-10)
            h_lin = jnp.einsum('bsh,oh->bso', h, W_lin[l]) + b_lin[l]
            ctx = jnp.matmul(attention, h_lin)
            h = jax.nn.relu(_layer_norm(ctx, ln_a[l], ln_b[l]))
        return h

    def _L2_gnn_ref(hidden_state, adjacency_matrix, Wl, bl, Ws, bs, Wr, br, ln_w, ln_b):
        import jax, jax.numpy as jnp
        import numpy as np
        LN_EPS = 1e-12

        def _digcn_forward(hidden_state, adjacency_matrix, Wl, bl, Ws, bs, Wr, br, ln_w, ln_b):
            B, S, D = hidden_state.shape
            temper = jnp.asarray(D, jnp.float32) ** 0.5
            i = jnp.arange(S)
            upper = (i[None, :] > i[:, None]).astype(hidden_state.dtype)
            lower = (i[None, :] < i[:, None]).astype(hidden_state.dtype)

            def layer(h, params):
                wl, b_l, ws, b_s, wr, b_r, g, beta = params
                u = jnp.einsum('bid,bjd->bij', h, h) / temper
                a = jax.nn.softmax(u, axis=-1)
                delta = a * adjacency_matrix
                attn = delta / (jnp.sum(delta, axis=-1, keepdims=True) + 1e-10)
                hl = h @ wl.T + b_l
                hs = h @ ws.T + b_s
                hr = h @ wr.T + b_r
                diag_a = jnp.diagonal(attn, axis1=1, axis2=2)
                ctx = jnp.einsum('bij,bjd->bid', attn * upper, hl) + diag_a[..., None] * hs + jnp.einsum('bij,bjd->bid', attn * lower, hr)
                mean = ctx.mean(-1, keepdims=True)
                var = ctx.var(-1, keepdims=True)
                o = (ctx - mean) / jnp.sqrt(var + LN_EPS) * g + beta
                return (jax.nn.relu(o), None)
            out, _ = jax.lax.scan(layer, hidden_state, (Wl, bl, Ws, bs, Wr, br, ln_w, ln_b))
            return out
        return _digcn_forward(hidden_state, adjacency_matrix, Wl, bl, Ws, bs, Wr, br, ln_w, ln_b)

    def _L3_gnn_ref(input_graph, adj, Wq, bq, Wk, bk, Wv, bv, beta):
        import jax, jax.numpy as jnp
        import numpy as np
        B, N, D, H = (8, 512, 384, 12)
        HD = D // H

        def _split_heads(x):
            b, n, _ = x.shape
            return x.reshape(b, n, H, HD).transpose(0, 2, 1, 3)
        q = _split_heads(input_graph @ Wq + bq)
        k = _split_heads(input_graph @ Wk + bk)
        v = _split_heads(input_graph @ Wv + bv)
        scores = jnp.einsum('bhqd,bhkd->bhqk', q, k) / jnp.sqrt(jnp.asarray(HD, input_graph.dtype))
        adj_e = adj[:, None, :, :]
        scores = scores + beta * adj_e
        scores = jnp.where(adj_e > 0, scores, jnp.asarray(-9000000000000000.0, scores.dtype))
        probs = jax.nn.softmax(scores, axis=-1)
        out = jnp.einsum('bhqk,bhkd->bhqd', probs, v)
        return out.transpose(0, 2, 1, 3).reshape(input_graph.shape[0], input_graph.shape[1], D)
    h = jnp.maximum(_layernorm(x, axis=-1), 0.0)
    x = x + _L0_gnn_ref(h, adj, L0_gnn_Wq, L0_gnn_Wk, L0_gnn_Wv, L0_gnn_bv, L0_gnn_Wo, L0_gnn_bo)
    h = jnp.maximum(_layernorm(x, axis=-1), 0.0)
    x = x + _L1_gnn_ref(h, adj, L1_gnn_W_left, L1_gnn_W_right, L1_gnn_W_lin, L1_gnn_b_lin, L1_gnn_ln_a, L1_gnn_ln_b)
    h = jnp.maximum(_layernorm(x, axis=-1), 0.0)
    x = x + _L2_gnn_ref(h, adj, L2_gnn_Wl, L2_gnn_bl, L2_gnn_Ws, L2_gnn_bs, L2_gnn_Wr, L2_gnn_br, L2_gnn_ln_w, L2_gnn_ln_b)
    h = jnp.maximum(_layernorm(x, axis=-1), 0.0)
    x = x + _L3_gnn_ref(h, adj, L3_gnn_Wq, L3_gnn_bq, L3_gnn_Wk, L3_gnn_bk, L3_gnn_Wv, L3_gnn_bv, L3_gnn_beta)
    return x

_drawn_inputs = setup_inputs


def setup_inputs(seed=0):
    import zlib

    import numpy as np

    out = dict(_drawn_inputs(seed))
    spreads = {'L1_gnn_b_lin': (0.0, 0.1),
     'L1_gnn_ln_a': (1.0, 0.2),
     'L1_gnn_ln_b': (0.0, 0.1),
     'L2_gnn_bl': (0.0, 0.457),
     'L2_gnn_bs': (0.0, 0.1),
     'L2_gnn_br': (0.0, 0.489),
     'L2_gnn_ln_w': (1.0, 0.2),
     'L2_gnn_ln_b': (0.0, 0.1),
     'L3_gnn_bq': (0.0, 0.8),
     'L3_gnn_bk': (0.0, 0.8),
     'L3_gnn_bv': (0.0, 0.1)}
    factors = {'L0_gnn_Wq': 3.864, 'L0_gnn_Wk': 3.827, 'L0_gnn_bv': 5.821, 'L0_gnn_bo': 6.936}
    for name, (base, spread) in spreads.items():
        noise = np.random.default_rng([zlib.crc32(name.encode()), seed]).standard_normal(out[name].shape)
        drawn = base * np.exp(spread * noise) if base else spread * noise
        out[name] = jnp.asarray(drawn.astype(out[name].dtype))
    for name, factor in factors.items():
        out[name] = (out[name] * factor).astype(out[name].dtype)
    return out
```

```python
from contextlib import ExitStack

import concourse.bass as bass
from concourse import mybir

F32 = mybir.dt.float32
F32R = mybir.dt.float32r
ALU = mybir.AluOpType
ACT = mybir.ActivationFunctionType
AX = mybir.AxisListType

P = 128
GRAPHS, NODES, D = 128, 64, 384
KC = D // P
ROWS = GRAPHS * NODES
TILES = 4
COLS = TILES * P
GROUPS = ROWS // COLS
HEADS, HD = 12, 32
PAIRS = HEADS // 2
HPC = P // HD
LN_EPS = 1e-5
SLOTS = 6
BIG = 9.0e15


def load_weights(sp, raw, weights, loaded):
    for s, w in enumerate(weights):
        sp.dma_start(raw[:, s], w.rearrange("(c p) n -> p c n", p=P)).then_inc(loaded, 16)


def split_matmul(nc, out, lhs, rhs, chunks=KC):
    n, last = 3 * chunks, None
    for c in range(chunks):
        for k, (a, b) in enumerate(((0, 0), (0, 1), (1, 0))):
            m = 3 * c + k
            last = nc.tensor.matmul(out, lhs[a](c), rhs[b](c), start=(m == 0), stop=(m == n - 1))
    return last


class Steps:

    def __init__(self, engine, sem, per):
        self.engine, self.sem, self.per, self.n, self.base = engine, sem, per, 0, 0

    def mark(self, instruction):
        instruction.then_inc(self.sem, 1)
        self.n += 1

    def catch_up(self):
        self.engine.wait_ge(self.sem, self.base + self.n)

    def done(self, instruction):
        self.mark(instruction)
        self.catch_up()

    def turn(self, i, before):
        if isinstance(i, int) and i == 0 and before == 0:
            self.base = 0
        else:
            self.base = i * self.per + before
        self.n = 0

    def ended(self):
        assert self.n == self.per, (self.n, self.per)


def attention_phase(nc, ctx, name, shared, x_in, adj_rows, x_out, biases, next_weights):
    proj = name == "l0"
    scale = float(D) ** -0.5 if proj else float(HD) ** -0.5
    w_hi, w_lo, raw, ident = shared["w_hi"], shared["w_lo"], shared["raw"], shared["ident"]
    n_w = 4 if proj else 3

    def sb(n, shape, dt=F32):
        return ctx.enter_context(nc.sbuf_tensor(f"{name}_{n}", shape, dt))

    def sem(n):
        return ctx.enter_context(nc.semaphore(f"{name}_{n}"))

    xl = sb("xl", [P, TILES, D])
    xr = sb("xr", [P, TILES, D])
    h = sb("h", [P, TILES, D])
    adj = sb("adj", [P, TILES, NODES])
    bias_qk = adj if proj else sb("score_bias", [P, TILES, NODES])
    masked = None if proj else sb("masked", [P, TILES, NODES])
    hT_hi = sb("hT_hi", [P, KC, COLS], F32R)
    hT_lo = sb("hT_lo", [P, KC, COLS], F32R)
    qT = sb("qT", [P, KC, COLS])
    kX = sb("kX", [P, KC, 2 * TILES, HPC, NODES])
    s_b = sb("s_b", [P, 2, HEADS, NODES])
    s_d = sb("s_d", [P, HEADS, NODES])
    e_x = sb("e_x", [P, HEADS * NODES])
    eT = sb("eT", [P, PAIRS, P])
    vX = sb("vX", [P, 2, 2, PAIRS, 2, HD + 1])
    o_rows = sb("o_rows", [P, 2, D])
    oT_hi = sb("oT_hi", [P, KC, P], F32R)
    oT_lo = sb("oT_lo", [P, KC, P], F32R)
    bv = sb("bv", [P, D])
    out_bias = sb("bo", [P, D]) if proj else bv
    b_q = sb("b_q", [P, KC])
    b_k = sb("b_k", [P, KC])
    beta = sb("beta", [P, 1])
    stats = sb("stats", [P, TILES, 6])
    pause = sb("pause", [P, 1])
    mv = sb("mv", [P, TILES, 2])
    var = sb("var", [P, TILES])
    half = sb("half", [P, TILES])
    rstd = sb("rstd", [P, TILES])
    nbias = sb("nbias", [P, TILES])
    mx = sb("mx", [P, 2, HEADS])
    mn = sb("mn", [P, 2, HEADS])
    most = sb("most", [P, HEADS])
    rs = sb("rs", [P, HEADS])

    psT = ctx.enter_context(nc.psum_tensor(f"{name}_psT", [P, 512], F32))
    psW = [ctx.enter_context(nc.psum_tensor(f"{name}_psW{b}", [P, 512], F32)) for b in range(2)]
    psS = ctx.enter_context(nc.psum_tensor(f"{name}_psS", [P, 2, 512], F32))
    psP = ctx.enter_context(nc.psum_tensor(f"{name}_psP", [P, 2, 512], F32))
    psO = ctx.enter_context(nc.psum_tensor(f"{name}_psO", [P, 512], F32))
    psQ = [psW[0], psW[0] if proj else psT, psW[0]]
    psK = [psW[1], psO, psW[1]]
    S_all = psS[:, :, :].rearrange("p a b -> p (a b)")[:, 0:HEADS * NODES]
    P_all = psP[:, :, :].rearrange("p a b -> p (a b)")[:, 0:PAIRS * P]
    O_all = psO[:, 0:HEADS * (HD + 1)].rearrange("p (h d) -> p h d", h=HEADS)

    w_hi_set = sem("w_hi_set")
    w_lo_set = sem("w_lo_set")
    zeroed = sem("zeroed")
    consts = sem("consts")
    xl_in = sem("xl_in")
    adj_in = sem("adj_in")
    xr_in = sem("xr_in")
    xr_set = sem("xr_set")
    bias_set = sem("bias_set")
    var_set = sem("var_set")
    rstd_set = sem("rstd_set")
    nbias_set = sem("nbias_set")
    h_set = sem("h_set")
    hT_done = sem("hT_done")
    hT_hi_set = sem("hT_hi_set")
    hT_set = sem("hT_set")
    q_done = sem("q_done")
    k_done = sem("k_done")
    q_set = sem("q_set")
    k_set = sem("k_set")
    s_done = sem("s_done")
    s_read = sem("s_read")
    mx_set = sem("mx_set")
    d_set = sem("d_set")
    e_set = sem("e_set")
    eT_done = sem("eT_done")
    eT_set = sem("eT_set")
    v_done = sem("v_done")
    v_set = sem("v_set")
    o_done = sem("o_done")
    o_set = sem("o_set")
    oT_done = sem("oT_done")
    oT_hi_set = sem("oT_hi_set")
    oT_set = sem("oT_set")
    y_done = sem("y_done")
    y_set = sem("y_set")
    stored = sem("stored")
    dve_step = sem("dve_step")

    def rows(ap, i):
        return ap[bass.ds(i * COLS, COLS), :].rearrange("(t p) n -> p t n", p=P)

    last = GROUPS - 1
    block = ctx.enter_context(nc.Block())

    @block.sync
    def _(sp):
        n_consts = 0
        for dst, src in biases(bv, out_bias, b_q, b_k, beta):
            sp.dma_start(dst, src).then_inc(consts, 16)
            n_consts += 1
        assert n_consts == (2 if proj else 4)
        sp.dma_start(xl[:], rows(x_in, 0)).then_inc(xl_in, 16)
        sp.dma_start(adj[:], rows(adj_rows, 0)).then_inc(adj_in, 16)
        sp.dma_start(xr[:], rows(x_in, 0)).then_inc(xr_in, 16)

        sp.wait_ge(h_set, TILES)
        sp.dma_start(xl[:], rows(x_in, 1)).then_inc(xl_in, 16)

        sp.wait_ge(w_lo_set, n_w)
        load_weights(sp, raw, next_weights, shared["w_loaded"])

        def turn(i, ahead, load_ahead=False):
            if load_ahead:
                sp.wait_ge(h_set, i * TILES + 2 * TILES)
                sp.dma_start(xl[:], rows(x_in, i + 2)).then_inc(xl_in, 16)
            for t in range(TILES):
                if t == 2 and ahead:
                    if proj:
                        sp.wait_ge(s_read, i * TILES + TILES)
                    else:
                        sp.wait_ge(bias_set, i + 1)
                    sp.dma_start(adj[:], rows(adj_rows, i + 1)).then_inc(adj_in, 16)
                sp.wait_ge(y_set, i * TILES + t + 1)
                sp.dma_start(x_out[bass.ds(i * COLS + t * P, P), :], xr[:, t, :]).then_inc(stored, 16)
            sp.wait_ge(stored, i * (16 * TILES) + 16 * TILES)
            if ahead:
                sp.dma_start(xr[:], rows(x_in, i + 1)).then_inc(xr_in, 16)

        with sp.Fori(0, last - 1) as i:
            turn(i, True, load_ahead=True)
        turn(last - 1, True)
        turn(last, False)

    @block.gpsimd
    def _(pool):
        nc.gpsimd.memset(kX[:], 0.0).then_inc(zeroed, 1)
        nc.gpsimd.memset(vX[:], 0.0).then_inc(zeroed, 1)
        nc.gpsimd.memset(half[:], -0.5).then_inc(zeroed, 1)
        pool.wait_ge(zeroed, 3)
        for b in range(2):
            nc.gpsimd.memset(vX[NODES * b:NODES * (b + 1), :, :, :, b, HD:HD + 1], 1.0).then_inc(zeroed, 1)

        def roots(i):
            pool.wait_ge(var_set, i + 1)
            nc.gpsimd.tensor_tensor(rstd[:], var[:], half[:], ALU.pow).then_inc(rstd_set, 1)

        pool.wait_ge(consts, 32 if proj else 64)
        roots(0)

        def less_maximum(i, t):
            pool.wait_ge(mx_set, i * TILES + t + 1)
            if t >= 1:
                pool.wait_ge(e_set, i * TILES + t)
            nc.gpsimd.tensor_tensor(s_d[:], s_b[:, t % 2],
                                    mx[:, t % 2, :].rearrange("p (h n) -> p h n", n=1).broadcast_to([P, HEADS, NODES]),
                                    ALU.subtract).then_inc(d_set, 1)

        def residual(i, t):
            if t == 0:
                pool.wait_ge(xr_in, i * 16 + 16)
            nc.gpsimd.tensor_tensor(xr[:, t, :], xr[:, t, :], out_bias[:], ALU.add).then_inc(xr_set, 1)

        def result(i, t):
            pool.wait_ge(xr_set, i * TILES + t + 1)
            pool.wait_ge(o_set, i * TILES + t + 1)
            nc.gpsimd.tensor_tensor(xr[:, t, :], xr[:, t, :], o_rows[:, t % 2, :], ALU.add).then_inc(y_set, 1)

        def turn(i, ahead):
            if ahead:
                roots(i + 1)
            for t in range(TILES):
                less_maximum(i, t)
                residual(i, t)
                if not proj and t >= 1:
                    result(i, t - 1)
            if not proj:
                result(i, TILES - 1)

        with pool.Fori(0, last) as i:
            turn(i, True)
        turn(last, False)

    @block.scalar
    def _(act):
        act.wait_ge(shared["w_loaded"], shared["w_count"][name])
        for s in range(n_w):
            nc.scalar.activation(w_hi[:, s], raw[:, s], ACT.Copy).then_inc(w_hi_set, 1)
        act.wait_ge(consts, 32 if proj else 64)
        act.wait_ge(zeroed, 5)

        def normalise(i, tiles=range(TILES)):
            act.wait_ge(nbias_set, i + 1)
            for t in tiles:
                nc.scalar.activation(h[:, t, :], xl[:, t, :], ACT.Relu, bias=nbias[:, t:t + 1],
                                     scale=rstd[:, t:t + 1]).then_inc(h_set, 1)

        def hT_parts(i, t):
            act.wait_ge(hT_done, i * TILES + t + 1)
            nc.scalar.activation(hT_hi[:, :, t * P:(t + 1) * P], psS[:, t % 2, 0:D].rearrange("p (c n) -> p c n", c=KC),
                                 ACT.Copy).then_inc(hT_hi_set, 1)

        def keys(i, c):
            act.wait_ge(k_done, i * KC + c + 1)
            for m in range(HPC):
                part = slice(HD * m, HD * (m + 1))
                src = psK[c][part, :].rearrange("p (g n) -> p g n", g=2 * TILES)
                if proj:
                    ins = nc.scalar.activation(kX[part, c, :, m, :], src, ACT.Copy)
                else:
                    ins = nc.scalar.activation(kX[part, c, :, m, :], src, ACT.Identity, bias=b_k[part, c:c + 1])
            ins.then_inc(k_set, 1)

        def exponentials(i, t):
            act.wait_ge(d_set, i * TILES + t + 1)
            nc.scalar.activation(e_x[:], s_d[:].rearrange("p h n -> p (h n)"), ACT.Exp).then_inc(e_set, 1)

        def values(i, t):
            act.wait_ge(v_done, i * TILES + t + 1)
            if t >= 2:
                act.wait_ge(o_done, i * TILES + t - 1)
            for g in range(2):
                for b in range(2):
                    part = slice(NODES * b, NODES * (b + 1))
                    src = psW[0][NODES * g:NODES * (g + 1), 0:D].rearrange("p (a b d) -> p a b d", b=2, d=HD)[:, :, b, :]
                    ins = nc.scalar.activation(vX[part, t % 2, g, :, b, 0:HD], src, ACT.Copy)
            ins.then_inc(v_set, 1)

        def eT_copy(i, t):
            act.wait_ge(eT_done, i * TILES + t + 1)
            nc.scalar.activation(eT[:, :, :].rearrange("p a n -> p (a n)"), P_all, ACT.Copy).then_inc(eT_set, 1)

        def oT_parts(i, t):
            act.wait_ge(oT_done, i * TILES + t + 1)
            nc.scalar.activation(oT_hi[:], psT[:, 0:D].rearrange("p (c n) -> p c n", c=KC), ACT.Copy)\
              .then_inc(oT_hi_set, 1)

        normalise(0)
        for t in range(TILES):
            hT_parts(0, t)
        for c in range(KC):
            keys(0, c)
        if not proj:
            values(0, 0)

        def turn(i, ahead):
            for t in range(TILES):
                if proj and t >= 2:
                    oT_parts(i, t - 2)
                if t >= 1:
                    eT_copy(i, t - 1)
                if not proj and t == 0:
                    values(i, 1)
                if ahead and t == TILES - 1:
                    hT_parts(i + 1, 0)
                    hT_parts(i + 1, 1)
                exponentials(i, t)
                if not proj and 1 <= t < TILES - 1:
                    values(i, t + 1)
                if t in (1, 2) and ahead:
                    normalise(i + 1, range(2 * (t - 1), 2 * t))
            if ahead and not proj:
                hT_parts(i + 1, 2)
                hT_parts(i + 1, 3)
            eT_copy(i, TILES - 1)
            if proj:
                oT_parts(i, TILES - 2)
            if ahead:
                if proj:
                    hT_parts(i + 1, 2)
                    hT_parts(i + 1, 3)
                if proj:
                    oT_parts(i, TILES - 1)
                for c in range(KC):
                    keys(i + 1, c)
                if not proj:
                    values(i + 1, 0)
            elif proj:
                oT_parts(i, TILES - 1)

        with act.Fori(0, last) as i:
            turn(i, True)
        turn(last, False)

    @block.vector
    def _(dve):
        step = Steps(dve, dve_step, 0)
        for s in range(n_w):
            dve.wait_ge(w_hi_set, s + 1)
            nc.vector.tensor_tensor(w_lo[:, s], raw[:, s], w_hi[:, s].bitcast(F32), ALU.subtract)\
              .then_inc(w_lo_set, 1)
        dve.wait_ge(consts, 32 if proj else 64)
        dve.wait_ge(zeroed, 5)

        def statistics(i):
            dve.wait_ge(xl_in, i * 16 + 16)
            for t in range(TILES):
                ins = nc.vector.bn_stats(stats[:, t, :], xl[:, t, :])
            step.done(ins)
            nc.vector.memset(pause[:], 0.0)
            for t in range(TILES):
                ins = nc.vector.bn_aggr(mv[:, t, :], stats[:, t, :])
            step.done(ins)
            nc.vector.tensor_scalar(var[:], mv[:, :, 1], LN_EPS, None, ALU.add).then_inc(var_set, 1)

        def shifts(i):
            dve.wait_ge(rstd_set, i + 1)
            nc.vector.scalar_tensor_tensor(nbias[:], mv[:, :, 0], -1.0, rstd[:], ALU.mult, ALU.mult)\
              .then_inc(nbias_set, 1)

        def hT_parts(i, t):
            dve.wait_ge(hT_hi_set, i * TILES + t + 1)
            cols = slice(t * P, (t + 1) * P)
            nc.vector.tensor_tensor(hT_lo[:, :, cols], psS[:, t % 2, 0:D].rearrange("p (c n) -> p c n", c=KC),
                                    hT_hi[:, :, cols].bitcast(F32), ALU.subtract).then_inc(hT_set, 1)

        def queries(i, c):
            dve.wait_ge(q_done, i * KC + c + 1)
            if proj:
                nc.vector.tensor_scalar(qT[:, c, :], psQ[c][:], scale, None, ALU.mult).then_inc(q_set, 1)
            else:
                nc.vector.tensor_scalar(qT[:, c, :], psQ[c][:], b_q[:, c:c + 1], scale, ALU.add, ALU.mult)\
                  .then_inc(q_set, 1)

        def score_bias(i):
            dve.wait_ge(adj_in, i * 16 + 16)
            step.done(nc.vector.tensor_scalar(masked[:], adj[:], 0.0, -BIG, ALU.is_le, ALU.mult))
            nc.vector.scalar_tensor_tensor(bias_qk[:], adj[:], beta[:], masked[:], ALU.mult, ALU.add)\
              .then_inc(bias_set, 1)

        def add_bias(i, t):
            if t == 0:
                if proj:
                    dve.wait_ge(adj_in, i * 16 + 16)
                else:
                    dve.wait_ge(bias_set, i + 1)
            dve.wait_ge(s_done, i * TILES + t + 1)
            if t >= 2:
                dve.wait_ge(d_set, i * TILES + t - 1)
            if proj and t >= 1:
                step.catch_up()
            nc.vector.tensor_tensor(s_b[:, t % 2], S_all.rearrange("p (h n) -> p h n", h=HEADS),
                                    bias_qk[:, t:t + 1, :].broadcast_to([P, HEADS, NODES]), ALU.add)\
              .then_inc(s_read, 1)

        def maximum(i, t):
            dve.wait_ge(s_read, i * TILES + t + 1)
            nc.vector.tensor_reduce(mx[:, t % 2, :], s_b[:, t % 2], axis=AX.X, op=ALU.max).then_inc(mx_set, 1)

        def least(i, t):
            step.mark(nc.vector.tensor_reduce(mn[:, t % 2, :], s_b[:, t % 2], axis=AX.X, op=ALU.min))

        def values(i, t):
            dve.wait_ge(v_done, i * TILES + t + 1)
            if t >= 2:
                dve.wait_ge(o_done, i * TILES + t - 1)
            for g in range(2):
                for b in range(2):
                    part = slice(NODES * b, NODES * (b + 1))
                    src = psW[0][NODES * g:NODES * (g + 1), 0:D].rearrange("p (a b d) -> p a b d", b=2, d=HD)[:, :, b, :]
                    bias = bv[part, :].rearrange("p (a b d) -> p a b d", b=2, d=HD)[:, :, b, :]
                    ins = nc.vector.tensor_tensor(vX[part, t % 2, g, :, b, 0:HD], src, bias, ALU.add)
            ins.then_inc(v_set, 1)

        def row_output(i, t):
            dve.wait_ge(o_done, i * TILES + t + 1)
            if not proj and t >= 2:
                dve.wait_ge(y_set, i * TILES + t - 1)
            if proj:
                dve.wait_ge(mx_set, i * TILES + t + 1)
                nc.vector.scalar_tensor_tensor(most[:], mn[:, t % 2, :], -1.0, mx[:, t % 2, :], ALU.mult, ALU.max)
            step.done(nc.vector.reciprocal(rs[:], O_all[:, :, HD]))
            if proj:
                step.done(nc.vector.scalar_tensor_tensor(rs[:], most[:], 0.0, rs[:], ALU.not_equal, ALU.mult))
            ins = nc.vector.tensor_tensor(o_rows[:, t % 2, :].rearrange("p (h d) -> p h d", h=HEADS), O_all[:, :, 0:HD],
                                          rs[:, :].rearrange("p (h n) -> p h n", n=1).broadcast_to([P, HEADS, HD]),
                                          ALU.mult)
            ins.then_inc(o_set, 1)

        def oT_parts(i, t):
            dve.wait_ge(oT_hi_set, i * TILES + t + 1)
            nc.vector.tensor_tensor(oT_lo[:], psT[:, 0:D].rearrange("p (c n) -> p c n", c=KC),
                                    oT_hi[:].bitcast(F32), ALU.subtract).then_inc(oT_set, 1)

        def result(i, t):
            dve.wait_ge(xr_set, i * TILES + t + 1)
            dve.wait_ge(y_done, i * TILES + t + 1)
            nc.vector.tensor_tensor(xr[:, t, :], psW[1][:, 0:D], xr[:, t, :], ALU.add).then_inc(y_set, 1)

        statistics(0)
        shifts(0)
        for t in range(TILES):
            hT_parts(0, t)
        for c in range(KC):
            queries(0, c)
        if not proj:
            score_bias(0)
        before = step.n
        step.per = 2 + TILES * 3 if proj else 3 + TILES

        def turn(i, ahead):
            step.turn(i, before)
            if ahead:
                statistics(i + 1)
            if proj:
                values(i, 0)
            for t in range(TILES):
                add_bias(i, t)
                if proj and t >= 2:
                    oT_parts(i, t - 2)
                maximum(i, t)
                if proj and t == 0:
                    values(i, 1)
                if proj and t >= 2:
                    result(i, t - 2)
                if proj:
                    least(i, t)
                if ahead and t == TILES - 1:
                    hT_parts(i + 1, 0)
                    hT_parts(i + 1, 1)
                if t >= 1:
                    row_output(i, t - 1)
                if proj and 1 <= t < TILES - 1:
                    values(i, t + 1)
                if t == 0 and ahead:
                    shifts(i + 1)
            if proj:
                oT_parts(i, TILES - 2)
            if ahead:
                hT_parts(i + 1, 2)
                hT_parts(i + 1, 3)
                if not proj:
                    score_bias(i + 1)
            row_output(i, TILES - 1)
            if proj:
                result(i, TILES - 2)
            if ahead:
                queries(i + 1, 0)
            if proj:
                oT_parts(i, TILES - 1)
            if ahead:
                queries(i + 1, 1)
            if proj:
                result(i, TILES - 1)
            if ahead:
                queries(i + 1, 2)

        with dve.Fori(0, last) as i:
            turn(i, True)
            step.ended()
        turn(last, False)

    @block.tensor
    def _(pe):
        pe.wait_ge(shared["ident_set"], 2)
        Q, K, V, O = range(4)

        def w_cols(s, cols):
            return tuple((lambda c, w=w: w[:, s, c, cols]) for w in (w_hi, w_lo))

        def h_cols(cols):
            return tuple((lambda c, x=x: x[:, c, cols]) for x in (hT_hi, hT_lo))

        def transposes(i, t):
            pe.wait_ge(h_set, i * TILES + t + 1)
            if t >= 2:
                pe.wait_ge(hT_set, i * TILES + t - 1)
            for c in range(KC):
                ins = nc.tensor.transpose(psS[:, t % 2, c * P:(c + 1) * P], h[:, t, c * P:(c + 1) * P], ident[:])
            ins.then_inc(hT_done, 1)

        def queries(i, c):
            if proj and c == 1 or c == 2:
                pe.wait_ge(q_set, i * KC + (c if proj else 1))
            split_matmul(nc, psQ[c][:], w_cols(Q, slice(c * P, (c + 1) * P)), h_cols(slice(0, COLS))).then_inc(q_done, 1)

        def keys(i, c):
            split_matmul(nc, psK[c][:], w_cols(K, slice(c * P, (c + 1) * P)), h_cols(slice(0, COLS))).then_inc(k_done, 1)

        def scores(i, t):
            if t == 0:
                pe.wait_ge(q_set, i * KC + KC)
                pe.wait_ge(hT_set, i * TILES + TILES)
            else:
                pe.wait_ge(s_read, i * TILES + t)
            for c in range(KC):
                if t == 0:
                    pe.wait_ge(k_set, i * KC + c + 1)
                for g in range(2):
                    lo = t * P + g * NODES
                    ins = nc.tensor.matmul(S_all[NODES * g:NODES * (g + 1), c * HPC * NODES:(c + 1) * HPC * NODES],
                                           qT[:, c, lo:lo + NODES], kX[:, c, 2 * t + g].rearrange("p h n -> p (h n)"),
                                           start=True, stop=True)
            ins.then_inc(s_done, 1)

        def values(i, t):
            if t == 0:
                pe.wait_ge(q_set, i * KC + KC)
            else:
                pe.wait_ge(v_set, i * TILES + t)
            split_matmul(nc, psW[0][:, 0:D], h_cols(slice(t * P, (t + 1) * P)), w_cols(V, slice(0, D))).then_inc(v_done, 1)

        def exp_transposes(i, t):
            pe.wait_ge(e_set, i * TILES + t + 1)
            for a in range(PAIRS):
                ins = nc.tensor.transpose(P_all[:, a * P:(a + 1) * P], e_x[:, a * P:(a + 1) * P], ident[:])
            ins.then_inc(eT_done, 1)

        def weigh(i, t):
            pe.wait_ge(eT_set, i * TILES + t + 1)
            pe.wait_ge(v_set, i * TILES + t + 1)
            if not proj and t >= 1:
                pe.wait_ge(o_set, i * TILES + t)
            for a in range(PAIRS):
                for g in range(2):
                    ins = nc.tensor.matmul(psO[NODES * g:NODES * (g + 1), a * 2 * (HD + 1):(a + 1) * 2 * (HD + 1)],
                                           eT[:, a, NODES * g:NODES * (g + 1)],
                                           vX[:, t % 2, g, a].rearrange("p b d -> p (b d)"), start=True, stop=True)
            ins.then_inc(o_done, 1)

        def out_transposes(i, t):
            pe.wait_ge(o_set, i * TILES + t + 1)
            for c in range(KC):
                ins = nc.tensor.transpose(psT[:, c * P:(c + 1) * P], o_rows[:, t % 2, c * P:(c + 1) * P], ident[:])
            ins.then_inc(oT_done, 1)

        def project(i, t, behind_keys=False):
            pe.wait_ge(oT_set, i * TILES + t + 1)
            if behind_keys:
                pe.wait_ge(k_set, i * KC + KC + 1)
            elif t >= 1:
                pe.wait_ge(y_set, i * TILES + t)
            oT = tuple((lambda c, x=x: x[:, c, :]) for x in (oT_hi, oT_lo))
            split_matmul(nc, psW[1][:, 0:D], oT, w_cols(O, slice(0, D))).then_inc(y_done, 1)

        def queries_and_keys(i, before_last=None):
            queries(i, 0)
            if before_last and proj:
                out_transposes(before_last[0], TILES - 1)
                pe.wait_ge(y_set, before_last[0] * TILES + TILES - 1)
            keys(i, 0)
            queries(i, 1)
            if before_last and proj:
                project(*before_last, behind_keys=True)
            queries(i, 2)
            if before_last and proj:
                pe.wait_ge(y_set, before_last[0] * TILES + TILES)
            if before_last:
                pe.wait_ge(o_set, before_last[0] * TILES + TILES)
            keys(i, 1)
            pe.wait_ge(k_set, i * KC + 1)
            keys(i, 2)
            values(i, 0)

        for t in range(TILES):
            transposes(0, t)
        pe.wait_ge(hT_set, TILES)
        pe.wait_ge(w_lo_set, n_w)
        queries_and_keys(0)

        def turn(i, ahead):
            for t in range(TILES):
                scores(i, t)
                if proj and t >= 2:
                    out_transposes(i, t - 2)
                if t < 2:
                    values(i, t + 1)
                if t >= 1:
                    exp_transposes(i, t - 1)
                if t == 2:
                    values(i, t + 1)
                if proj and t >= 2:
                    project(i, t - 2)
                if ahead and t == TILES - 1:
                    pe.wait_ge(s_read, i * TILES + TILES)
                    transposes(i + 1, 0)
                    transposes(i + 1, 1)
                if t >= 1:
                    weigh(i, t - 1)
            if ahead and not proj:
                transposes(i + 1, 2)
                transposes(i + 1, 3)
            exp_transposes(i, TILES - 1)
            if proj:
                out_transposes(i, TILES - 2)
            if ahead and proj:
                transposes(i + 1, 2)
                transposes(i + 1, 3)
            weigh(i, TILES - 1)
            if proj:
                project(i, TILES - 2)
            if ahead:
                pe.wait_ge(v_set, i * TILES + TILES)
                pe.wait_ge(hT_set, i * TILES + 2 * TILES)
                queries_and_keys(i + 1, (i, TILES - 1))
            elif proj:
                out_transposes(i, TILES - 1)
                project(i, TILES - 1)

        with pe.Fori(0, last) as i:
            turn(i, True)
        turn(last, False)


def bilinear_phase(nc, ctx, shared, x_in, adj, x_out, a, next_weights):
    w_hi, w_lo, raw, ident = shared["w_hi"], shared["w_lo"], shared["raw"], shared["ident"]
    n_w = 6
    eps, var_scale = 1e-3, float(D) / (D - 1)

    def sb(n, shape, dt=F32):
        return ctx.enter_context(nc.sbuf_tensor(f"l1_{n}", shape, dt))

    def ps(n):
        return ctx.enter_context(nc.psum_tensor(f"l1_{n}", [P, 512], F32))

    def sem(n):
        return ctx.enter_context(nc.semaphore(f"l1_{n}"))

    xl = sb("xl", [P, TILES, D])
    xr = sb("xr", [P, TILES, D])
    h = sb("h", [P, TILES, D])
    hT = [(sb(f"hT{k}_hi", [P, KC, COLS], F32R), sb(f"hT{k}_lo", [P, KC, COLS], F32R)) for k in range(4)]
    m_hi = sb("m_hi", [P, 2, KC, COLS], F32R)
    m_lo = sb("m_lo", [P, 2, KC, COLS], F32R)
    adj_bd = sb("adj_bd", [P, TILES, P])
    adjT = [sb(f"adjT{g}", [P, TILES, P]) for g in range(2)]
    masks = [sb(f"masks{g}", [P, TILES, 2, P]) for g in range(2)]
    tri = sb("tri", [P, 2, P])
    u_parts = sb("u_parts", [P, 2, P])
    u_sum = sb("u_sum", [P, P])
    e_u = sb("e_u", [P, P])
    dT = sb("dT", [P, 2, P])
    lin = sb("lin", [P, 2, D + 1])
    act_rows = sb("act_rows", [P, 2, D])
    b_lin, ln_a, ln_b = (sb(n, [P, 2, D]) for n in ("b_lin", "ln_a", "ln_b"))
    half = sb("half", [P, 2])
    stats = sb("stats", [P, TILES, 6])
    pause = sb("pause", [P, 1])
    mv = sb("mv", [P, TILES, 2])
    var = sb("var", [P, TILES])
    rstd = sb("rstd", [P, TILES])
    nbias = sb("nbias", [P, TILES])
    c_sum, c_r, c_var, c_root, c_inv, c_scale, c_nb = (sb(n, [P, TILES]) for n in (
        "c_sum", "c_r", "c_var", "c_root", "c_inv", "c_scale", "c_nb"))
    c_stats = sb("c_stats", [P, TILES, 6])
    c_mv = sb("c_mv", [P, TILES, 2])

    psU, psX = ps("psU"), ps("psX")
    psW, psC, psT = ([ps(f"{n}{b}") for b in range(2)] for n in ("psW", "psC", "psT"))

    w_hi_set = sem("w_hi_set")
    w_lo_set = sem("w_lo_set")
    zeroed = sem("zeroed")
    consts = sem("consts")
    xl_in = sem("xl_in")
    adj_in = sem("adj_in")
    xr_in = sem("xr_in")
    var_set = sem("var_set")
    rstd_set = sem("rstd_set")
    nbias_set = sem("nbias_set")
    h_set = sem("h_set")
    hT_done = sem("hT_done")
    hT_hi_set = sem("hT_hi_set")
    hT_set = sem("hT_set")
    m_done = sem("m_done")
    m_hi_set = sem("m_hi_set")
    m_set = sem("m_set")
    adjT_done = sem("adjT_done")
    adjT_set = sem("adjT_set")
    masks_set = sem("masks_set")
    u_done = sem("u_done")
    u_set = sem("u_set")
    e_set = sem("e_set")
    d_set = sem("d_set")
    lin_done = sem("lin_done")
    lin_set = sem("lin_set")
    c_done = sem("c_done")
    c_var_set = sem("c_var_set")
    c_root_set = sem("c_root_set")
    c_ln_set = sem("c_ln_set")
    rows_set = sem("rows_set")
    affine_set = sem("affine_set")
    y_set = sem("y_set")
    stored = sem("stored")
    dve_step = sem("dve_step")
    pool_step = sem("pool_step")

    def rows(ap, q):
        return ap[bass.ds(q * COLS, COLS), :].rearrange("(t p) n -> p t n", p=P)

    turns = GROUPS // 2
    last = turns - 1
    block = ctx.enter_context(nc.Block())

    @block.sync
    def _(sp):
        for dst, name in ((b_lin, "L1_gnn_b_lin"), (ln_a, "L1_gnn_ln_a"), (ln_b, "L1_gnn_ln_b")):
            sp.dma_start(dst[:], a[name].partition_broadcast(P)).then_inc(consts, 16)

        def load_adj(q):
            graphs = adj[bass.ds(q * 2 * TILES, 2 * TILES), :, :].rearrange("(t g) i j -> g i t j", g=2)
            for g in range(2):
                sp.dma_start(adj_bd[NODES * g:NODES * (g + 1), :, NODES * g:NODES * (g + 1)], graphs[g])\
                  .then_inc(adj_in, 16)

        def store(i, k):
            for t in range(TILES):
                sp.wait_ge(y_set, (2 * i + k - 2) * TILES + t + 1)
                sp.dma_start(x_out[bass.ds((2 * i + k - 2) * COLS + t * P, P), :], xr[:, t, :]).then_inc(stored, 16)
            sp.wait_ge(stored, (2 * i + k - 1) * (16 * TILES))

        sp.dma_start(xl[:], rows(x_in, 0)).then_inc(xl_in, 16)
        sp.dma_start(xr[:], rows(x_in, 0)).then_inc(xr_in, 16)
        sp.wait_ge(zeroed, 1)
        load_adj(0)
        sp.wait_ge(h_set, TILES)
        sp.dma_start(xl[:], rows(x_in, 1)).then_inc(xl_in, 16)
        sp.wait_ge(w_lo_set, n_w)
        load_weights(sp, raw, next_weights, shared["w_loaded"])

        def turn(i, ahead):
            sp.wait_ge(masks_set, 2 * (2 * i + 1))
            sp.wait_ge(adjT_done, 2 * i + 1)
            load_adj(2 * i + 1)
            if ahead:
                sp.wait_ge(h_set, (2 * i + 2) * TILES)
                sp.dma_start(xl[:], rows(x_in, 2 * i + 2)).then_inc(xl_in, 16)
                sp.wait_ge(masks_set, 2 * (2 * i + 2))
                sp.wait_ge(adjT_done, 2 * i + 2)
                load_adj(2 * i + 2)
                sp.wait_ge(h_set, (2 * i + 3) * TILES)
                sp.dma_start(xl[:], rows(x_in, 2 * i + 3)).then_inc(xl_in, 16)
            store(i, 2)
            sp.dma_start(xr[:], rows(x_in, 2 * i + 1)).then_inc(xr_in, 16)
            store(i, 3)
            if ahead:
                sp.dma_start(xr[:], rows(x_in, 2 * i + 2)).then_inc(xr_in, 16)

        with sp.Fori(0, last) as i:
            turn(i, True)
        turn(last, False)

    @block.gpsimd
    def _(pool):
        step = Steps(pool, pool_step, 4 * TILES)
        nc.gpsimd.memset(adj_bd[:], 0.0).then_inc(zeroed, 1)
        nc.gpsimd.memset(half[:, 0:1], -0.5).then_inc(zeroed, 1)
        nc.gpsimd.memset(half[:, 1:2], 0.5).then_inc(zeroed, 1)
        nc.gpsimd.memset(lin[:, :, D:D + 1], 1.0).then_inc(zeroed, 1)
        nc.gpsimd.memset(tri[:], 1.0).then_inc(zeroed, 1)
        pool.wait_ge(zeroed, 5)
        nc.gpsimd.affine_select(out=tri[:, 0, :], in_=tri[:, 0, :], compare_op=ALU.is_ge, fill=0.0, base=0,
                                pattern=[[-1, P]], channel_multiplier=1).then_inc(zeroed, 1)
        nc.gpsimd.affine_select(out=tri[:, 1, :], in_=tri[:, 1, :], compare_op=ALU.is_gt, fill=0.0, base=0,
                                pattern=[[1, P]], channel_multiplier=-1).then_inc(zeroed, 1)
        pool.wait_ge(zeroed, 7)
        pool.wait_ge(consts, 48)

        def roots(q):
            pool.wait_ge(var_set, q + 1)
            nc.gpsimd.tensor_tensor(rstd[:], var[:], half[:, 0:1].broadcast_to([P, TILES]), ALU.pow).then_inc(rstd_set, 1)

        def make_masks(q, g):
            pool.wait_ge(adjT_set, q + 1)
            nc.gpsimd.tensor_tensor(masks[g][:, :, 0, :], adjT[g][:], tri[:, 0:1, :].broadcast_to([P, TILES, P]),
                                    ALU.mult).then_inc(masks_set, 1)
            nc.gpsimd.tensor_tensor(masks[g][:, :, 1, :], adj_bd[:], tri[:, 1:2, :].broadcast_to([P, TILES, P]),
                                    ALU.mult).then_inc(masks_set, 1)

        def root(i, k, t):
            pool.wait_ge(c_var_set, (4 * i + k) * TILES + t + 1)
            nc.gpsimd.tensor_tensor(c_root[:, t:t + 1], c_var[:, t:t + 1], half[:, 1:2], ALU.pow).then_inc(c_root_set, 1)

        def affine(i, k, t):
            pool.wait_ge(rows_set, (4 * i + k) * TILES + t + 1)
            row = act_rows[:, t % 2, :]
            step.done(nc.gpsimd.tensor_tensor(row, row, ln_a[:, k // 2, :], ALU.mult))
            nc.gpsimd.tensor_tensor(row, row, ln_b[:, k // 2, :], ALU.add).then_inc(affine_set, 1)

        def unit(i, k, ahead):
            for t in range(TILES):
                if t >= 2:
                    affine(i, k, t - 2)
                if t >= 1:
                    root(i, k, t - 1)
            if k == 0:
                make_masks(2 * i + 1, 1)
            if k == 3 and ahead:
                make_masks(2 * i + 2, 0)
            affine(i, k, 2)
            root(i, k, 3)
            affine(i, k, 3)
            if ahead and k in (1, 2):
                roots(2 * i + k + 1)

        roots(0)
        roots(1)
        make_masks(0, 0)

        def turn(i, ahead):
            step.turn(i, 0)
            for k in range(4):
                unit(i, k, ahead)

        with pool.Fori(0, last) as i:
            turn(i, True)
            step.ended()
        turn(last, False)

    @block.scalar
    def _(act):
        act.wait_ge(shared["w_loaded"], shared["w_count"]["l1"])
        for s in range(n_w):
            nc.scalar.activation(w_hi[:, s], raw[:, s], ACT.Copy).then_inc(w_hi_set, 1)

        def normalise(q):
            act.wait_ge(nbias_set, q + 1)
            for t in range(TILES):
                nc.scalar.activation(h[:, t, :], xl[:, t, :], ACT.Relu, bias=nbias[:, t:t + 1],
                                     scale=rstd[:, t:t + 1]).then_inc(h_set, 1)

        def hT_part(index, k, t):
            act.wait_ge(hT_done, index + 1)
            nc.scalar.activation(hT[k][0][:, :, t * P:(t + 1) * P],
                                 psT[t % 2][:, 0:D].rearrange("p (c n) -> p c n", c=KC), ACT.Relu).then_inc(hT_hi_set, 1)

        def m_part(i, k, j):
            act.wait_ge(m_done, (4 * i + k) * 2 * KC + j + 1)
            nc.scalar.activation(m_hi[:, j // KC, j % KC, :], psW[j % 2][:], ACT.Copy).then_inc(m_hi_set, 1)

        def exponential(i, k, t):
            act.wait_ge(u_set, (4 * i + k) * TILES + t + 1)
            nc.scalar.activation(e_u[:], u_sum[:], ACT.Exp, scale=float(D) ** -0.5).then_inc(e_set, 1)

        def norm_rows(i, k, t):
            act.wait_ge(c_ln_set, (4 * i + k) * TILES + t + 1)
            nc.scalar.activation(act_rows[:, t % 2, :], psC[t % 2][:, 0:D], ACT.Identity, bias=c_nb[:, t:t + 1],
                                 scale=c_scale[:, t:t + 1]).then_inc(rows_set, 1)

        def adjT_copy(q, g):
            act.wait_ge(adjT_done, q + 1)
            nc.scalar.activation(adjT[g][:].rearrange("p t n -> p (t n)"), psX[:], ACT.Copy).then_inc(adjT_set, 1)

        def products(i, k, tail):
            def left(f, t):
                if tail:
                    f(*tail, t)

            def left_T(t):
                if tail and tail[1] < 2:
                    hT_part(2 * TILES + (4 * tail[0] + tail[1]) * TILES + t, tail[1] + 2, t)

            m_part(i, k, 0)
            left(norm_rows, 2)
            m_part(i, k, 1)
            left_T(1)
            m_part(i, k, 2)
            left(norm_rows, 3)
            left_T(2)
            m_part(i, k, 3)
            m_part(i, k, 4)
            left_T(3)
            m_part(i, k, 5)

        def unit(i, k, ahead):
            for t in range(TILES):
                exponential(i, k, t)
                if t >= 2:
                    norm_rows(i, k, t - 2)
                if k < 2 and t == 3:
                    hT_part(2 * TILES + (4 * i + k) * TILES, k + 2, 0)
                if k >= 2 and ahead:
                    hT_part(2 * TILES + (4 * i + k) * TILES + t, k - 2, t)
            if k == 0:
                adjT_copy(2 * i + 1, 1)
            if k == 3 and ahead:
                adjT_copy(2 * i + 2, 0)
            if k < 3:
                products(i, k + 1, (i, k))
                if ahead and k in (1, 2):
                    normalise(2 * i + k + 1)
            elif ahead:
                products(i + 1, 0, (i, 3))
            else:
                norm_rows(i, k, 2)
                norm_rows(i, k, 3)

        for q in range(2):
            normalise(q)
            for t in range(TILES):
                hT_part(q * TILES + t, q, t)
        adjT_copy(0, 0)
        products(0, 0, None)

        def turn(i, ahead):
            for k in range(4):
                unit(i, k, ahead)

        with act.Fori(0, last) as i:
            turn(i, True)
        turn(last, False)

    @block.vector
    def _(dve):
        step = Steps(dve, dve_step, 0)
        for s in range(n_w):
            dve.wait_ge(w_hi_set, s + 1)
            nc.vector.tensor_tensor(w_lo[:, s], raw[:, s], w_hi[:, s].bitcast(F32), ALU.subtract).then_inc(w_lo_set, 1)
        dve.wait_ge(consts, 48)
        dve.wait_ge(zeroed, 7)

        def statistics(q):
            dve.wait_ge(xl_in, q * 16 + 16)
            for t in range(TILES):
                ins = nc.vector.bn_stats(stats[:, t, :], xl[:, t, :])
            step.done(ins)
            nc.vector.memset(pause[:], 0.0)
            for t in range(TILES):
                ins = nc.vector.bn_aggr(mv[:, t, :], stats[:, t, :])
            step.done(ins)
            nc.vector.tensor_scalar(var[:], mv[:, :, 1], LN_EPS, None, ALU.add).then_inc(var_set, 1)

        def shifts(q):
            dve.wait_ge(rstd_set, q + 1)
            nc.vector.scalar_tensor_tensor(nbias[:], mv[:, :, 0], -1.0, rstd[:], ALU.mult, ALU.mult)\
              .then_inc(nbias_set, 1)

        def hT_part(index, k, t):
            dve.wait_ge(hT_hi_set, index + 1)
            hi, lo = (x[:, :, t * P:(t + 1) * P] for x in hT[k])
            nc.vector.scalar_tensor_tensor(lo, psT[t % 2][:, 0:D].rearrange("p (c n) -> p c n", c=KC), 0.0,
                                           hi.bitcast(F32), ALU.max, ALU.subtract).then_inc(hT_set, 1)

        def m_part(i, k, j):
            dve.wait_ge(m_hi_set, (4 * i + k) * 2 * KC + j + 1)
            nc.vector.tensor_tensor(m_lo[:, j // KC, j % KC, :], psW[j % 2][:], m_hi[:, j // KC, j % KC, :].bitcast(F32),
                                    ALU.subtract).then_inc(m_set, 1)

        def mask_u(i, k, t):
            if t == 0:
                dve.wait_ge(masks_set, 2 * (2 * i + k % 2 + 1))
            dve.wait_ge(u_done, (4 * i + k) * TILES + t + 1)
            step.done(nc.vector.tensor_tensor(u_parts[:], psU[:, 0:2 * P].rearrange("p (s n) -> p s n", s=2),
                                              masks[k % 2][:, t], ALU.mult))
            nc.vector.tensor_tensor(u_sum[:], u_parts[:, 0, :], u_parts[:, 1, :], ALU.add).then_inc(u_set, 1)

        def lin_copy(i, k, t):
            dve.wait_ge(lin_done, (4 * i + k) * TILES + t + 1)
            nc.vector.tensor_tensor(lin[:, t % 2, 0:D], psW[t % 2][:, 0:D], b_lin[:, k // 2, :], ALU.add)\
              .then_inc(lin_set, 1)

        def weigh_adj(i, k, t):
            dve.wait_ge(e_set, (4 * i + k) * TILES + t + 1)
            nc.vector.tensor_tensor(dT[:, t % 2, :], e_u[:], adjT[k % 2][:, t, :], ALU.mult).then_inc(d_set, 1)

        def context_statistics(i, k, t):
            dve.wait_ge(c_done, (4 * i + k) * TILES + t + 1)
            one = slice(t, t + 1)
            step.mark(nc.vector.tensor_scalar(c_sum[:, one], psC[t % 2][:, D:D + 1], 1e-10, None, ALU.add))
            step.done(nc.vector.bn_stats(c_stats[:, t, :], psC[t % 2][:, 0:D]))
            step.mark(nc.vector.reciprocal(c_r[:, one], c_sum[:, one]))
            step.done(nc.vector.bn_aggr(c_mv[:, t, :], c_stats[:, t, :]))
            nc.vector.tensor_scalar(c_var[:, one], c_mv[:, t, 1:2], c_r[:, one], c_r[:, one], ALU.mult, ALU.mult)\
              .then_inc(c_var_set, 1)

        def context_norm(i, k, t):
            dve.wait_ge(c_root_set, (4 * i + k) * TILES + t + 1)
            one = slice(t, t + 1)
            step.done(nc.vector.tensor_scalar(c_inv[:, one], c_root[:, one], var_scale ** 0.5, eps, ALU.mult, ALU.add))
            step.done(nc.vector.reciprocal(c_inv[:, one], c_inv[:, one]))
            step.done(nc.vector.tensor_tensor(c_scale[:, one], c_inv[:, one], c_r[:, one], ALU.mult))
            nc.vector.scalar_tensor_tensor(c_nb[:, one], c_mv[:, t, 0:1], -1.0, c_scale[:, one], ALU.mult, ALU.mult)\
              .then_inc(c_ln_set, 1)

        def result(i, k, t):
            if t == 0:
                dve.wait_ge(xr_in, (2 * i + k - 1) * 16)
            dve.wait_ge(affine_set, (4 * i + k) * TILES + t + 1)
            nc.vector.scalar_tensor_tensor(xr[:, t, :], act_rows[:, t % 2, :], 0.0, xr[:, t, :], ALU.max, ALU.add)\
              .then_inc(y_set, 1)

        def products(i, k, tail, q):
            def left(f, t):
                if tail:
                    f(*tail, t)

            def left_end(t):
                if tail and tail[1] < 2:
                    hT_part(2 * TILES + (4 * tail[0] + tail[1]) * TILES + t, tail[1] + 2, t)
                elif tail:
                    result(*tail, t)

            m_part(i, k, 0)
            left(context_norm, 2)
            left(context_statistics, 3)
            m_part(i, k, 1)
            left_end(1)
            m_part(i, k, 2)
            left(context_norm, 3)
            left_end(2)
            m_part(i, k, 3)
            m_part(i, k, 4)
            left_end(3)
            if q is not None:
                statistics(q)
            m_part(i, k, 5)
            if q is not None:
                shifts(q)

        def unit(i, k, ahead):
            for t in range(TILES):
                mask_u(i, k, t)
                if t >= 2:
                    context_norm(i, k, t - 2)
                lin_copy(i, k, t)
                weigh_adj(i, k, t)
                if t >= 1:
                    context_statistics(i, k, t - 1)
                if k < 2 and t == 3:
                    hT_part(2 * TILES + (4 * i + k) * TILES, k + 2, 0)
                if k >= 2 and ahead:
                    hT_part(2 * TILES + (4 * i + k) * TILES + t, k - 2, t)
                if k >= 2 and t == 3:
                    result(i, k, 0)
            if k < 3:
                products(i, k + 1, (i, k), 2 * i + k + 1 if ahead and k in (1, 2) else None)
            elif ahead:
                products(i + 1, 0, (i, 3), None)
            else:
                context_norm(i, k, 2)
                context_statistics(i, k, 3)
                result(i, k, 1)
                context_norm(i, k, 3)
                result(i, k, 2)
                result(i, k, 3)

        for q in range(2):
            statistics(q)
            shifts(q)
            for t in range(TILES):
                hT_part(q * TILES + t, q, t)
        products(0, 0, None, None)
        before = step.n
        step.per = 4 * TILES * 8 + 2 * 2

        def turn(i, ahead):
            step.turn(i, before)
            for k in range(4):
                unit(i, k, ahead)

        with dve.Fori(0, last) as i:
            turn(i, True)
            step.ended()
        turn(last, False)

    @block.tensor
    def _(pe):
        pe.wait_ge(shared["ident_set"], 2)
        LEFT, RIGHT, LIN = range(3)

        def w_cols(layer, s, cols):
            return tuple((lambda c, w=w: w[:, 3 * layer + s, c, cols]) for w in (w_hi, w_lo))

        def h_cols(k, t=None):
            cols = slice(0, COLS) if t is None else slice(t * P, (t + 1) * P)
            return tuple((lambda c, x=x: x[:, c, cols]) for x in hT[k])

        def transposes(index, src, t):
            for c in range(KC):
                ins = nc.tensor.transpose(psT[t % 2][:, c * P:(c + 1) * P], src[:, c * P:(c + 1) * P], ident[:])
            ins.then_inc(hT_done, 1)

        def first_transposes(q, index, t):
            pe.wait_ge(h_set, q * TILES + t + 1)
            if not isinstance(index, int) or index >= 2:
                pe.wait_ge(hT_set, index - 1)
            transposes(index, h[:, t, :], t)

        def next_transposes(i, k, t):
            index = 2 * TILES + (4 * i + k) * TILES + t
            pe.wait_ge(affine_set, (4 * i + k) * TILES + t + 1)
            pe.wait_ge(hT_set, index - 1)
            transposes(index, act_rows[:, t % 2, :], t)

        def adj_transposes(q):
            pe.wait_ge(adj_in, 32 * (q + 1))
            if not (isinstance(q, int) and q == 0):
                pe.wait_ge(adjT_set, q)
            for t in range(TILES):
                ins = nc.tensor.transpose(psX[:, t * P:(t + 1) * P], adj_bd[:, t, :], ident[:])
            ins.then_inc(adjT_done, 1)

        def product(i, k, j):
            if j >= 2:
                pe.wait_ge(m_set, (4 * i + k) * 2 * KC + j - 1)
            s, c = (LEFT, RIGHT)[j // KC], j % KC
            split_matmul(nc, psW[j % 2][:], w_cols(k // 2, s, slice(c * P, (c + 1) * P)), h_cols(k)).then_inc(m_done, 1)

        def bilinear(i, k, t):
            n = (4 * i + k) * TILES + t
            if t == 0:
                pe.wait_ge(m_set, (4 * i + k + 1) * 2 * KC)
            else:
                pe.wait_ge(u_set, n)
            for s in range(2):
                m = tuple((lambda c, x=x, s=s: x[:, s, c, t * P:(t + 1) * P]) for x in (m_hi, m_lo))
                ins = split_matmul(nc, psU[:, s * P:(s + 1) * P], m, h_cols(k, t))
            ins.then_inc(u_done, 1)

        def linear(i, k, t):
            n = (4 * i + k) * TILES + t
            if t >= 2:
                pe.wait_ge(lin_set, n - 1)
            split_matmul(nc, psW[t % 2][:, 0:D], h_cols(k, t), w_cols(k // 2, LIN, slice(0, D))).then_inc(lin_done, 1)

        def context(i, k, t):
            n = (4 * i + k) * TILES + t
            pe.wait_ge(d_set, n + 1)
            pe.wait_ge(lin_set, n + 1)
            if t >= 2:
                pe.wait_ge(rows_set, n - 1)
            nc.tensor.matmul(psC[t % 2][:, 0:D + 1], dT[:, t % 2, :], lin[:, t % 2, :], start=True, stop=True)\
              .then_inc(c_done, 1)

        def products(i, k, tail):
            def left_T(t):
                if tail and tail[1] < 2:
                    next_transposes(*tail, t)

            if tail:
                pe.wait_ge(lin_set, (4 * tail[0] + tail[1] + 1) * TILES)
            product(i, k, 0)
            if tail:
                context(*tail, 3)
            product(i, k, 1)
            left_T(1)
            product(i, k, 2)
            left_T(2)
            product(i, k, 3)
            product(i, k, 4)
            left_T(3)
            product(i, k, 5)
            if tail:
                pe.wait_ge(rows_set, (4 * tail[0] + tail[1] + 1) * TILES)

        def unit(i, k, ahead):
            for t in range(TILES):
                bilinear(i, k, t)
                linear(i, k, t)
                if t >= 1:
                    context(i, k, t - 1)
                if k < 2 and t == 3:
                    next_transposes(i, k, 0)
                if k >= 2 and ahead:
                    first_transposes(2 * i + k, 2 * TILES + (4 * i + k) * TILES + t, t)
            if k == 0:
                adj_transposes(2 * i + 1)
            if k == 3 and ahead:
                adj_transposes(2 * i + 2)
            if k < 3:
                products(i, k + 1, (i, k))
            elif ahead:
                products(i + 1, 0, (i, 3))
            else:
                context(i, k, 3)

        for q in range(2):
            for t in range(TILES):
                first_transposes(q, q * TILES + t, t)
        adj_transposes(0)
        pe.wait_ge(hT_set, 2 * TILES)
        pe.wait_ge(w_lo_set, n_w)
        products(0, 0, None)

        def turn(i, ahead):
            for k in range(4):
                unit(i, k, ahead)

        with pe.Fori(0, last) as i:
            turn(i, True)
        turn(last, False)


def directed_phase(nc, ctx, shared, x_in, adj, x_out, a, next_weights):
    w_hi, w_lo, raw, ident = shared["w_hi"], shared["w_lo"], shared["raw"], shared["ident"]
    n_w = 6
    temper = float(D) ** -0.5

    def sb(n, shape, dt=F32):
        return ctx.enter_context(nc.sbuf_tensor(f"l2_{n}", shape, dt))

    def ps(n):
        return ctx.enter_context(nc.psum_tensor(f"l2_{n}", [P, 512], F32))

    def sem(n):
        return ctx.enter_context(nc.semaphore(f"l2_{n}"))

    xl = sb("xl", [P, TILES, D])
    xr = [sb(f"xr{g}", [P, TILES, D]) for g in range(2)]
    h = sb("h", [P, TILES, D])
    hT = [(sb(f"hT{k}_hi", [P, KC, COLS], F32R), sb(f"hT{k}_lo", [P, KC, COLS], F32R)) for k in range(4)]
    adj_rows = [sb(f"adj{g}", [P, TILES, NODES]) for g in range(2)]
    mx = sb("mx", [P, TILES])
    s_u = sb("s_u", [P, TILES, NODES])
    e_u = sb("e_u", [P, TILES, NODES])
    delta = sb("delta", [P, TILES, NODES])
    delta_diag = sb("delta_diag", [P, TILES, NODES])
    delta_bd = sb("delta_bd", [P, TILES, P])
    z_sum, d_sum = sb("z_sum", [P, TILES]), sb("d_sum", [P, TILES])
    own = sb("own", [P, 2, TILES])
    r = sb("r", [P, 2, TILES])
    tri = sb("tri", [P, 2, P])
    eye = sb("eye", [P, NODES])
    dT = sb("dT", [P, TILES, 2, P])
    sides = sb("sides", [P, 2, 2, D])
    selves = sb("selves", [P, 2, D])
    con = sb("con", [P, TILES, D])
    b_l, b_r, b_s, ln_w, ln_b = (sb(n, [P, 2, D]) for n in ("b_l", "b_r", "b_s", "ln_w", "ln_b"))
    half = sb("half", [P, 1])
    stats = sb("stats", [P, TILES, 6])
    pause = sb("pause", [P, 1])
    mv = sb("mv", [P, TILES, 2])
    var = sb("var", [P, TILES])
    rstd = sb("rstd", [P, TILES])
    nbias = sb("nbias", [P, TILES])
    c_r2, c_var, c_root, c_scale, c_nb = (sb(n, [P, TILES]) for n in ("c_r2", "c_var", "c_root", "c_scale", "c_nb"))
    c_stats = sb("c_stats", [P, TILES, 6])
    c_mv = sb("c_mv", [P, TILES, 2])

    psU, psE, psC = ps("psU"), ps("psE"), ps("psC")
    psW = [ps(f"psW{b}") for b in range(3)]
    psT = [ps(f"psT{b}") for b in range(2)]

    w_hi_set = sem("w_hi_set")
    w_lo_set = sem("w_lo_set")
    zeroed = sem("zeroed")
    consts = sem("consts")
    xl_in = sem("xl_in")
    adj_in = [sem(f"adj_in{g}") for g in range(2)]
    xr_in = [sem(f"xr_in{g}") for g in range(2)]
    stored = [sem(f"stored{g}") for g in range(2)]
    var_set = sem("var_set")
    rstd_set = sem("rstd_set")
    nbias_set = sem("nbias_set")
    h_set = sem("h_set")
    hT_done = sem("hT_done")
    hT_hi_set = sem("hT_hi_set")
    hT_set = sem("hT_set")
    u_done = sem("u_done")
    s_set = sem("s_set")
    e_set = sem("e_set")
    delta_set = sem("delta_set")
    diag_set = sem("diag_set")
    bd_set = sem("bd_set")
    dT_done = sem("dT_done")
    dT_set = sem("dT_set")
    side_done = sem("side_done")
    side_set = sem("side_set")
    self_done = sem("self_done")
    self_set = sem("self_set")
    c_done = sem("c_done")
    c_set = sem("c_set")
    c_var_set = sem("c_var_set")
    c_root_set = sem("c_root_set")
    c_ln_set = sem("c_ln_set")
    norm_set = sem("norm_set")
    affine_set = sem("affine_set")
    y_set = sem("y_set")
    dve_step = sem("dve_step")
    pool_step = sem("pool_step")

    def rows(ap, q):
        return ap[bass.ds(q * COLS, COLS), :].rearrange("(t p) n -> p t n", p=P)

    def T_index(i, k, t):
        return 2 * TILES + (4 * i + k) * TILES + t

    JOBS = {(0, 3): [(0, 0)],
            (1, 0): [(0, 1)], (1, 1): [(0, 2)], (1, 2): [(0, 3)], (1, 3): [(1, 0)],
            (2, 0): [(1, 1)], (2, 1): [(1, 2)], (2, 2): [(1, 3)], (2, 3): [(2, 0), (2, 1)],
            (3, 0): [(2, 2), (2, 3)], (3, 2): [(3, 0), (3, 1)], (3, 3): [(3, 2), (3, 3)]}

    def jobs(k, t, ahead):
        return [(source, x) for source, x in JOBS.get((k, t), []) if source < 2 or ahead]

    turns = GROUPS // 2
    last = turns - 1
    block = ctx.enter_context(nc.Block())

    @block.sync
    def _(sp):
        vectors = ((b_l, "L2_gnn_bl"), (b_r, "L2_gnn_br"), (b_s, "L2_gnn_bs"), (ln_w, "L2_gnn_ln_w"), (ln_b, "L2_gnn_ln_b"))
        for dst, name in vectors:
            sp.dma_start(dst[:], a[name].partition_broadcast(P)).then_inc(consts, 16)
        adj_flat = adj.rearrange("b q k -> (b q) k")
        sp.dma_start(xl[:], rows(x_in, 0)).then_inc(xl_in, 16)
        for g in range(2):
            sp.dma_start(adj_rows[g][:], rows(adj_flat, g)).then_inc(adj_in[g], 16)
            sp.dma_start(xr[g][:], rows(x_in, g)).then_inc(xr_in[g], 16)
        sp.wait_ge(h_set, TILES)
        sp.dma_start(xl[:], rows(x_in, 1)).then_inc(xl_in, 16)
        sp.wait_ge(w_lo_set, n_w)
        load_weights(sp, raw, next_weights, shared["w_loaded"])

        def store(i, g, ahead):
            for t in range(TILES):
                sp.wait_ge(y_set, (2 * i + g) * TILES + t + 1)
                sp.dma_start(x_out[bass.ds((2 * i + g) * COLS + t * P, P), :], xr[g][:, t, :]).then_inc(stored[g], 16)
            sp.wait_ge(stored[g], (i + 1) * (16 * TILES))
            if ahead:
                sp.dma_start(xr[g][:], rows(x_in, 2 * i + 2 + g)).then_inc(xr_in[g], 16)

        def turn(i, ahead):
            if ahead:
                sp.wait_ge(h_set, (2 * i + 2) * TILES)
                sp.dma_start(xl[:], rows(x_in, 2 * i + 2)).then_inc(xl_in, 16)
                for g in range(2):
                    sp.wait_ge(delta_set, 4 * i + 3 + g)
                    sp.wait_ge(s_set, 4 * i + 3 + g)
                    sp.dma_start(adj_rows[g][:], rows(adj_flat, 2 * i + 2 + g)).then_inc(adj_in[g], 16)
                sp.wait_ge(h_set, (2 * i + 3) * TILES)
                sp.dma_start(xl[:], rows(x_in, 2 * i + 3)).then_inc(xl_in, 16)
            store(i, 0, ahead)
            store(i, 1, ahead)

        with sp.Fori(0, last) as i:
            turn(i, True)
        turn(last, False)

    @block.gpsimd
    def _(pool):
        step = Steps(pool, pool_step, 4 * TILES)
        pool.wait_ge(shared["ident_set"], 2)
        nc.gpsimd.memset(delta_bd[:], 0.0).then_inc(zeroed, 1)
        nc.gpsimd.memset(half[:], -0.5).then_inc(zeroed, 1)
        nc.gpsimd.memset(tri[:], 1.0).then_inc(zeroed, 1)
        nc.gpsimd.tensor_tensor(eye[:], ident[:, 0:NODES], ident[:, NODES:P], ALU.add).then_inc(zeroed, 1)
        pool.wait_ge(zeroed, 4)
        for s, sign in enumerate((1, -1)):
            nc.gpsimd.affine_select(out=tri[:, s, :], in_=tri[:, s, :], compare_op=ALU.is_gt, fill=0.0, base=0,
                                    pattern=[[-sign, P]], channel_multiplier=sign).then_inc(zeroed, 1)
        pool.wait_ge(zeroed, 6)
        pool.wait_ge(consts, 80)

        def roots(q):
            pool.wait_ge(var_set, q + 1)
            nc.gpsimd.tensor_tensor(rstd[:], var[:], half[:].broadcast_to([P, TILES]), ALU.pow).then_inc(rstd_set, 1)

        def diagonal(i, k):
            pool.wait_ge(delta_set, 4 * i + k + 1)
            nc.gpsimd.tensor_tensor(delta_diag[:], delta[:], eye[:].rearrange("p (t n) -> p t n", t=1)
                                    .broadcast_to([P, TILES, NODES]), ALU.mult).then_inc(diag_set, 1)

        def root(i, k, t):
            pool.wait_ge(c_var_set, (4 * i + k) * TILES + t + 1)
            nc.gpsimd.tensor_tensor(c_root[:, t:t + 1], c_var[:, t:t + 1], half[:], ALU.pow).then_inc(c_root_set, 1)

        def affine(i, k, t):
            pool.wait_ge(norm_set, (4 * i + k) * TILES + t + 1)
            step.done(nc.gpsimd.tensor_tensor(con[:, t, :], con[:, t, :], ln_w[:, k // 2, :], ALU.mult))
            nc.gpsimd.tensor_tensor(con[:, t, :], con[:, t, :], ln_b[:, k // 2, :], ALU.add).then_inc(affine_set, 1)

        roots(0)
        roots(1)
        diagonal(0, 0)

        def turn(i, ahead):
            step.turn(i, 0)
            for k in range(4):
                if k >= 2 and ahead:
                    roots(2 * i + k)
                root(i, k, 0)
                affine(i, k, 0)
                root(i, k, 1)
                affine(i, k, 1)
                root(i, k, 2)
                if k < 3:
                    diagonal(i, k + 1)
                elif ahead:
                    diagonal(i + 1, 0)
                root(i, k, 3)
                affine(i, k, 2)
                affine(i, k, 3)

        with pool.Fori(0, last) as i:
            turn(i, True)
            step.ended()
        turn(last, False)

    @block.scalar
    def _(act):
        act.wait_ge(shared["w_loaded"], shared["w_count"]["l2"])
        for s in range(n_w):
            nc.scalar.activation(w_hi[:, s], raw[:, s], ACT.Copy).then_inc(w_hi_set, 1)
        act.wait_ge(zeroed, 6)

        def normalise(q):
            act.wait_ge(nbias_set, q + 1)
            for t in range(TILES):
                nc.scalar.activation(h[:, t, :], xl[:, t, :], ACT.Relu, bias=nbias[:, t:t + 1],
                                     scale=rstd[:, t:t + 1]).then_inc(h_set, 1)

        def hT_part(index, unit, t):
            act.wait_ge(hT_done, index + 1)
            nc.scalar.activation(hT[unit][0][:, :, t * P:(t + 1) * P],
                                 psT[t % 2][:, 0:D].rearrange("p (c n) -> p c n", c=KC), ACT.Relu).then_inc(hT_hi_set, 1)

        def exponential(i, k):
            act.wait_ge(s_set, 4 * i + k + 1)
            nc.scalar.activation(e_u[:], s_u[:], ACT.Exp, scale=temper).then_inc(e_set, 1)

        def block_diagonal(i, k):
            act.wait_ge(delta_set, 4 * i + k + 1)
            for g in range(2):
                part = slice(NODES * g, NODES * (g + 1))
                nc.scalar.activation(delta_bd[part, :, part], delta[part], ACT.Copy).then_inc(bd_set, 1)

        def norm_rows(i, k, t):
            act.wait_ge(c_ln_set, (4 * i + k) * TILES + t + 1)
            nc.scalar.activation(con[:, t, :], con[:, t, :], ACT.Identity, bias=c_nb[:, t:t + 1],
                                 scale=c_scale[:, t:t + 1]).then_inc(norm_set, 1)

        def slot(i, k, t, ahead):
            if t >= 2:
                norm_rows(i, k, t - 2)
            if t == 3 and (k < 3 or ahead):
                following = (i, k + 1) if k < 3 else (i + 1, 0)
                exponential(*following)
                block_diagonal(*following)
            if t == 3:
                norm_rows(i, k, 2)
            for source, x in jobs(k, t, ahead):
                hT_part(T_index(i, source, x), (source + 2) % 4, x)
            if ahead and (k, t) in ((2, 2), (3, 1)):
                normalise(2 * i + k)
            if t == 3:
                norm_rows(i, k, 3)

        for q in range(2):
            normalise(q)
            for t in range(TILES):
                hT_part(q * TILES + t, q, t)
        exponential(0, 0)
        block_diagonal(0, 0)

        def turn(i, ahead):
            for k in range(4):
                for t in range(TILES):
                    slot(i, k, t, ahead)

        with act.Fori(0, last) as i:
            turn(i, True)
        turn(last, False)

    @block.vector
    def _(dve):
        step = Steps(dve, dve_step, 0)
        for s in range(n_w):
            dve.wait_ge(w_hi_set, s + 1)
            nc.vector.tensor_tensor(w_lo[:, s], raw[:, s], w_hi[:, s].bitcast(F32), ALU.subtract).then_inc(w_lo_set, 1)
        dve.wait_ge(consts, 80)
        dve.wait_ge(zeroed, 6)

        def statistics(q):
            dve.wait_ge(xl_in, q * 16 + 16)
            for t in range(TILES):
                ins = nc.vector.bn_stats(stats[:, t, :], xl[:, t, :])
            step.done(ins)
            nc.vector.memset(pause[:], 0.0)
            for t in range(TILES):
                ins = nc.vector.bn_aggr(mv[:, t, :], stats[:, t, :])
            step.done(ins)
            nc.vector.tensor_scalar(var[:], mv[:, :, 1], LN_EPS, None, ALU.add).then_inc(var_set, 1)

        def shifts(q):
            dve.wait_ge(rstd_set, q + 1)
            nc.vector.scalar_tensor_tensor(nbias[:], mv[:, :, 0], -1.0, rstd[:], ALU.mult, ALU.mult)\
              .then_inc(nbias_set, 1)

        def hT_part(index, unit, t):
            dve.wait_ge(hT_hi_set, index + 1)
            hi, lo = (x[:, :, t * P:(t + 1) * P] for x in hT[unit])
            nc.vector.scalar_tensor_tensor(lo, psT[t % 2][:, 0:D].rearrange("p (c n) -> p c n", c=KC), 0.0,
                                           hi.bitcast(F32), ALU.max, ALU.subtract).then_inc(hT_set, 1)

        def less_maximum(i, k):
            dve.wait_ge(u_done, 4 * i + k + 1)
            u = psU[:].rearrange("p (t n) -> p t n", t=TILES)
            for g in range(2):
                part = slice(NODES * g, NODES * (g + 1))
                step.mark(nc.vector.tensor_reduce(mx[part, :], u[part, :, part], axis=AX.X, op=ALU.max))
            step.catch_up()
            for g in range(2):
                part = slice(NODES * g, NODES * (g + 1))
                most = mx[part, :].rearrange("p (t n) -> p t n", n=1).broadcast_to([NODES, TILES, NODES])
                ins = nc.vector.tensor_tensor(s_u[part], u[part, :, part], most, ALU.subtract)
            ins.then_inc(s_set, 1)

        def row_factors(i, k):
            dve.wait_ge(e_set, 4 * i + k + 1)
            dve.wait_ge(adj_in[k % 2], (i + 1) * 16)
            nc.vector.tensor_tensor(delta[:], e_u[:], adj_rows[k % 2][:], ALU.mult).then_inc(delta_set, 1)
            step.mark(nc.vector.tensor_reduce(z_sum[:], e_u[:], axis=AX.X, op=ALU.add))
            dve.wait_ge(delta_set, 4 * i + k + 1)
            step.done(nc.vector.tensor_reduce(d_sum[:], delta[:], axis=AX.X, op=ALU.add))
            step.done(nc.vector.scalar_tensor_tensor(r[:, k % 2, :], z_sum[:], 1e-10, d_sum[:], ALU.mult, ALU.add))
            step.mark(nc.vector.reciprocal(r[:, k % 2, :], r[:, k % 2, :]))
            dve.wait_ge(diag_set, 4 * i + k + 1)
            step.done(nc.vector.tensor_reduce(own[:, k % 2, :], delta_diag[:], axis=AX.X, op=ALU.add))

        def attention_parts(i, k):
            dve.wait_ge(dT_done, 4 * i + k + 1)
            whole = psE[:].rearrange("p (t s n) -> p t s n", t=TILES, s=1).broadcast_to([P, TILES, 2, P])
            side = tri[:].rearrange("p (t s) n -> p t s n", t=1).broadcast_to([P, TILES, 2, P])
            nc.vector.tensor_tensor(dT[:], whole, side, ALU.mult).then_inc(dT_set, 1)

        def side_copy(i, k, t, s):
            n = (4 * i + k) * TILES + t
            dve.wait_ge(side_done, 2 * n + s + 1)
            nc.vector.tensor_tensor(sides[:, t % 2, s, :], psW[s][:, 0:D], (b_l, b_r)[s][:, k // 2, :], ALU.add)\
              .then_inc(side_set, 1)

        def self_copy(i, k, t):
            dve.wait_ge(self_done, (4 * i + k) * TILES + t + 1)
            nc.vector.tensor_tensor(selves[:, t % 2, :], psW[2][:, 0:D], b_s[:, k // 2, :], ALU.add).then_inc(self_set, 1)

        def context(i, k, t):
            n = (4 * i + k) * TILES + t
            one = slice(t, t + 1)
            dve.wait_ge(c_done, n + 1)
            dve.wait_ge(self_set, n + 1)
            nc.vector.scalar_tensor_tensor(con[:, t, :], selves[:, t % 2, :], own[:, k % 2, one], psC[:, 0:D],
                                           ALU.mult, ALU.add).then_inc(c_set, 1)
            dve.wait_ge(c_set, n + 1)
            step.done(nc.vector.bn_stats(c_stats[:, t, :], con[:, t, :]))
            nc.vector.tensor_tensor(c_r2[:, one], r[:, k % 2, one], r[:, k % 2, one], ALU.mult)
            step.done(nc.vector.bn_aggr(c_mv[:, t, :], c_stats[:, t, :]))
            nc.vector.tensor_scalar(c_var[:, one], c_mv[:, t, 1:2], c_r2[:, one], 1e-12, ALU.mult, ALU.add)\
              .then_inc(c_var_set, 1)

        def context_norm(i, k, t):
            one = slice(t, t + 1)
            dve.wait_ge(c_root_set, (4 * i + k) * TILES + t + 1)
            step.done(nc.vector.tensor_tensor(c_scale[:, one], c_root[:, one], r[:, k % 2, one], ALU.mult))
            nc.vector.scalar_tensor_tensor(c_nb[:, one], c_mv[:, t, 0:1], -1.0, c_scale[:, one], ALU.mult, ALU.mult)\
              .then_inc(c_ln_set, 1)

        def result(i, k, t):
            g = k - 2
            if t == 0:
                dve.wait_ge(xr_in[g], (i + 1) * 16)
            dve.wait_ge(affine_set, (4 * i + k) * TILES + t + 1)
            nc.vector.scalar_tensor_tensor(xr[g][:, t, :], con[:, t, :], 0.0, xr[g][:, t, :], ALU.max, ALU.add)\
              .then_inc(y_set, 1)

        def slot(i, k, t, ahead):
            if t >= 2:
                context_norm(i, k, t - 2)
            side_copy(i, k, t, 0)
            if ahead and (k, t) == (3, 1):
                shifts(2 * i + 3)
            side_copy(i, k, t, 1)
            if t == 0:
                attention_parts(i, k)
            self_copy(i, k, t)
            following = (i, k + 1) if k < 3 else (i + 1, 0)
            if t == 3 and (k < 3 or ahead):
                less_maximum(*following)
            if t >= 1:
                context(i, k, t - 1)
            if t == 3:
                if k < 3 or ahead:
                    row_factors(*following)
                context_norm(i, k, 2)
            for source, x in jobs(k, t, ahead):
                hT_part(T_index(i, source, x), (source + 2) % 4, x)
            if k == 3 and t < 3:
                result(i, 2, t + 1)
            if k >= 2 and t == 3:
                result(i, k, 0)
            if ahead and (k, t) in ((2, 0), (3, 0)):
                statistics(2 * i + k)
            if ahead and (k, t) == (2, 1):
                shifts(2 * i + 2)
            if t == 3:
                context(i, k, 3)
                context_norm(i, k, 3)
            if k == 3 and t == 3:
                for x in range(1, TILES):
                    result(i, 3, x)

        for q in range(2):
            statistics(q)
            shifts(q)
            for t in range(TILES):
                hT_part(q * TILES + t, q, t)
        less_maximum(0, 0)
        row_factors(0, 0)
        before = step.n
        step.per = 4 * (2 + 5 + TILES * (2 + 1)) + 2 * 2

        def turn(i, ahead):
            step.turn(i, before)
            for k in range(4):
                for t in range(TILES):
                    slot(i, k, t, ahead)

        with dve.Fori(0, last) as i:
            turn(i, True)
            step.ended()
        turn(last, False)

    @block.tensor
    def _(pe):
        pe.wait_ge(shared["ident_set"], 2)
        LEFT, RIGHT, SELF = range(3)

        def h_cols(k, t):
            return tuple((lambda c, x=x: x[:, c, t * P:(t + 1) * P]) for x in hT[k])

        def projection(k, s):
            return tuple((lambda c, w=w: w[:, 3 * (k // 2) + s, c, :]) for w in (w_hi, w_lo))

        def transposes(index, src, t):
            if not (isinstance(index, int) and index < 2):
                pe.wait_ge(hT_set, index - 1)
            for c in range(KC):
                ins = nc.tensor.transpose(psT[t % 2][:, c * P:(c + 1) * P], src[:, c * P:(c + 1) * P], ident[:])
            ins.then_inc(hT_done, 1)

        def products(i, k):
            pe.wait_ge(hT_set, (4 * i + (0, 2, 3, 4)[k]) * TILES + (1 if k == 0 else 0) * TILES)
            if not (isinstance(i, int) and i == 0 and k == 0):
                pe.wait_ge(s_set, 4 * i + k)
            for t in range(TILES):
                ins = split_matmul(nc, psU[:, t * P:(t + 1) * P], h_cols(k, t), h_cols(k, t))
            ins.then_inc(u_done, 1)

        def delta_transposes(i, k):
            pe.wait_ge(bd_set, 2 * (4 * i + k + 1))
            for t in range(TILES):
                ins = nc.tensor.transpose(psE[:, t * P:(t + 1) * P], delta_bd[:, t, :], ident[:])
            ins.then_inc(dT_done, 1)

        def side(i, k, t, s):
            n = (4 * i + k) * TILES + t
            if t >= 1:
                pe.wait_ge(side_set, 2 * n - 1 + s)
            split_matmul(nc, psW[s][:, 0:D], h_cols(k, t), projection(k, s)).then_inc(side_done, 1)

        def self_part(i, k, t):
            n = (4 * i + k) * TILES + t
            if t >= 1:
                pe.wait_ge(self_set, n)
            split_matmul(nc, psW[2][:, 0:D], h_cols(k, t), projection(k, SELF)).then_inc(self_done, 1)

        def context(i, k, t):
            n = (4 * i + k) * TILES + t
            if t == 0:
                pe.wait_ge(dT_set, 4 * i + k + 1)
            else:
                pe.wait_ge(c_set, n)
            pe.wait_ge(side_set, 2 * n + 2)
            for s in range(2):
                ins = nc.tensor.matmul(psC[:, 0:D], dT[:, t, s, :], sides[:, t % 2, s, :], start=(s == 0), stop=(s == 1))
            ins.then_inc(c_done, 1)

        def slot(i, k, t, ahead):
            side(i, k, t, 0)
            side(i, k, t, 1)
            if t == 0:
                delta_transposes(i, k)
            self_part(i, k, t)
            if t == 3 and k < 3:
                products(i, k + 1)
            elif t == 3 and ahead:
                products(i + 1, 0)
            if t >= 1:
                context(i, k, t - 1)
            for source, x in jobs(k, t, ahead):
                if source < 2:
                    pe.wait_ge(affine_set, (4 * i + source) * TILES + x + 1)
                    transposes(T_index(i, source, x), con[:, x, :], x)
                else:
                    pe.wait_ge(h_set, (2 * i + source) * TILES + x + 1)
                    transposes(T_index(i, source, x), h[:, x, :], x)
            if t == 3:
                context(i, k, 3)
                pe.wait_ge(self_set, (4 * i + k + 1) * TILES)

        for q in range(2):
            for t in range(TILES):
                pe.wait_ge(h_set, q * TILES + t + 1)
                transposes(q * TILES + t, h[:, t, :], t)
        products(0, 0)
        pe.wait_ge(w_lo_set, n_w)

        def turn(i, ahead):
            for k in range(4):
                for t in range(TILES):
                    slot(i, k, t, ahead)

        with pe.Fori(0, last) as i:
            turn(i, True)
        turn(last, False)


PHASE_WEIGHTS = {
    "l0": ["L0_gnn_Wq", "L0_gnn_Wk", "L0_gnn_Wv", "L0_gnn_Wo"],
    "l1": ["L1_gnn_W_left0", "L1_gnn_W_right0", "L1_gnn_W_lin0", "L1_gnn_W_left1", "L1_gnn_W_right1", "L1_gnn_W_lin1"],
    "l2": ["L2_gnn_Wl0", "L2_gnn_Wr0", "L2_gnn_Ws0", "L2_gnn_Wl1", "L2_gnn_Wr1", "L2_gnn_Ws1"],
    "l3": ["L3_gnn_Wq", "L3_gnn_Wk", "L3_gnn_Wv"],
}
PHASES = ["l0", "l1", "l2", "l3"]


def build(nc, a, out, phases=PHASES):
    x = a["x"].rearrange("b n d -> (b n) d")
    adj_rows = a["adj"].rearrange("b q k -> (b q) k")
    out_rows = out.rearrange("b n d -> (b n) d")
    graph_phase = {"l1": bilinear_phase, "l2": directed_phase}
    with ExitStack() as ctx:
        shared = {
            "w_hi": ctx.enter_context(nc.sbuf_tensor("w_hi", [P, SLOTS, KC, D], F32R)),
            "w_lo": ctx.enter_context(nc.sbuf_tensor("w_lo", [P, SLOTS, KC, D], F32R)),
            "raw": ctx.enter_context(nc.sbuf_tensor("w_raw", [P, SLOTS, KC, D], F32)),
            "ident": ctx.enter_context(nc.sbuf_tensor("ident", [P, P], F32)),
            "w_loaded": ctx.enter_context(nc.semaphore("w_loaded")),
            "ident_set": ctx.enter_context(nc.semaphore("ident_set")),
            "w_count": {},
        }
        n = 0
        for name in phases:
            n += 16 * len(PHASE_WEIGHTS[name])
            shared["w_count"][name] = n
        weights = {name: [a[w] for w in PHASE_WEIGHTS[name]] for name in phases}

        with nc.Block() as block:
            @block.sync
            def _(sp):
                load_weights(sp, shared["raw"], weights[phases[0]], shared["w_loaded"])

            @block.gpsimd
            def _(pool):
                ident = shared["ident"]
                nc.gpsimd.memset(ident[:], 0.0).then_inc(shared["ident_set"], 1)
                pool.wait_ge(shared["ident_set"], 1)
                nc.gpsimd.affine_select(out=ident[:], in_=ident[:], compare_op=ALU.not_equal, fill=1.0, base=0,
                                        pattern=[[-1, P]], channel_multiplier=1).then_inc(shared["ident_set"], 1)

        def across(v):
            return v.partition_broadcast(P)

        source = x
        for k, name in enumerate(phases):
            last = k == len(phases) - 1
            target = out_rows if last else nc.dram_tensor(f"after_{name}", (ROWS, D), F32, kind="Internal").ap()
            following = [] if last else weights[phases[k + 1]]
            with ExitStack() as phase:
                if name == "l0":
                    def biases(bv, bo, b_q, b_k, beta):
                        return [(bv[:], across(a["L0_gnn_bv"])), (bo[:], across(a["L0_gnn_bo"]))]
                    attention_phase(nc, phase, name, shared, source, adj_rows, target, biases, following)
                elif name == "l3":
                    def biases(bv, bo, b_q, b_k, beta):
                        return [(bv[:], across(a["L3_gnn_bv"])), (b_q[:], a["L3_gnn_bq"]), (b_k[:], a["L3_gnn_bk"]),
                                (beta[:], a["L3_gnn_beta"].partition_broadcast(P))]
                    attention_phase(nc, phase, name, shared, source, adj_rows, target, biases, following)
                else:
                    graph_phase[name](nc, phase, shared, source, a["adj"], target, a, following)
            source = target


def laid_out(inputs):
    import numpy as np

    arrays = {}
    for n, v in inputs.items():
        v = np.ascontiguousarray(v)
        if n == "L3_gnn_beta":
            arrays[n] = v.reshape(1)
        elif n in ("L3_gnn_bq", "L3_gnn_bk"):
            arrays[n] = np.ascontiguousarray(v.reshape(KC, P).T)
        elif n in ("L0_gnn_Wq", "L0_gnn_Wk", "L0_gnn_Wv", "L0_gnn_Wo"):
            arrays[n] = np.ascontiguousarray(v.T)
        elif n in ("L1_gnn_W_left", "L1_gnn_W_right", "L1_gnn_W_lin", "L2_gnn_Wl", "L2_gnn_Wr", "L2_gnn_Ws"):
            for layer in range(2):
                arrays[f"{n}{layer}"] = np.ascontiguousarray(v[layer].T)
        else:
            arrays[n] = v
    return arrays


def kernel(**inputs):
    import concourse.bacc as bacc
    from concourse.bass_utils import run_bass_kernel_spmd

    arrays = laid_out(inputs)
    nc = bacc.Bacc("TRN2", target_bir_lowering=False, num_devices=1)
    a = {n: nc.dram_tensor(f"in_{n}", v.shape, mybir.dt.from_np(v.dtype), kind="ExternalInput").ap()
         for n, v in arrays.items()}
    out = nc.dram_tensor("out_x", (GRAPHS, NODES, D), F32, kind="ExternalOutput").ap()
    build(nc, a, out)
    r = run_bass_kernel_spmd(nc, [{f"in_{n}": v for n, v in arrays.items()}], core_ids=[0])
    return r.results[0]["out_x"]
```

```python
from contextlib import ExitStack

import concourse.bass as bass
from concourse import mybir

F32 = mybir.dt.float32
F32R = mybir.dt.float32r
ALU = mybir.AluOpType
ACT = mybir.ActivationFunctionType
AX = mybir.AxisListType

P = 128
GRAPHS, NODES, D = 128, 64, 384
KC = D // P
ROWS = GRAPHS * NODES
TILES = 4
COLS = TILES * P
GROUPS = ROWS // COLS
HEADS, HD = 12, 32
PAIRS = HEADS // 2
HPC = P // HD
LN_EPS = 1e-5
SLOTS = 6
BIG = 9.0e15


def load_weights(sp, raw, weights, loaded):
    for s, w in enumerate(weights):
        sp.dma_start(raw[:, s], w.rearrange("(c p) n -> p c n", p=P)).then_inc(loaded, 16)


def split_matmul(nc, out, lhs, rhs, chunks=KC):
    n, last = 3 * chunks, None
    for c in range(chunks):
        for k, (a, b) in enumerate(((0, 0), (0, 1), (1, 0))):
            m = 3 * c + k
            last = nc.tensor.matmul(out, lhs[a](c), rhs[b](c), start=(m == 0), stop=(m == n - 1))
    return last


class Steps:

    def __init__(self, engine, sem, per):
        self.engine, self.sem, self.per, self.n, self.base = engine, sem, per, 0, 0

    def mark(self, instruction):
        instruction.then_inc(self.sem, 1)
        self.n += 1
        return self.n

    def catch_up(self, n=None):
        self.engine.wait_ge(self.sem, self.base + (self.n if n is None else n))

    def done(self, instruction):
        self.mark(instruction)
        self.catch_up()

    def turn(self, i, before):
        if isinstance(i, int) and i == 0 and before == 0:
            self.base = 0
        else:
            self.base = i * self.per + before
        self.n = 0

    def ended(self):
        assert self.n == self.per, (self.n, self.per)


def attention_phase(nc, ctx, name, shared, x_in, adj_rows, x_out, biases, own_weights, next_weights):
    proj = name == "l0"
    scale = float(D) ** -0.5 if proj else float(HD) ** -0.5
    w_hi, w_lo, raw, ident = shared["w_hi"], shared["w_lo"], shared["raw"], shared["ident"]
    n_w = 4 if proj else 3

    def sb(n, shape, dt=F32):
        return ctx.enter_context(nc.sbuf_tensor(f"{name}_{n}", shape, dt))

    def sem(n):
        return ctx.enter_context(nc.semaphore(f"{name}_{n}"))

    xl = sb("xl", [P, TILES, D])
    xr = sb("xr", [P, TILES, D])
    h = sb("h", [P, TILES, D])
    adj = sb("adj", [P, TILES, NODES])
    bias_qk = adj if proj else sb("score_bias", [P, TILES, NODES])
    masked = None if proj else sb("masked", [P, TILES, NODES])
    hT_hi = sb("hT_hi", [P, KC, COLS], F32R)
    hT_lo = sb("hT_lo", [P, KC, COLS], F32R)
    qT = sb("qT", [P, KC, COLS])
    kX = sb("kX", [P, KC, 2 * TILES, HPC, NODES])
    s_b = sb("s_b", [P, 2, HEADS, NODES])
    s_d = sb("s_d", [P, HEADS, NODES])
    e_x = sb("e_x", [P, HEADS * NODES])
    eT = sb("eT", [P, PAIRS, P])
    vX = sb("vX", [P, 2, 2, PAIRS, 2, HD + 1])
    o_rows = sb("o_rows", [P, 2, D])
    y_rows = sb("y_rows", [P, 2, D]) if proj else o_rows
    oT_hi = sb("oT_hi", [P, KC, P], F32R)
    oT_lo = sb("oT_lo", [P, KC, P], F32R)
    bv = sb("bv", [P, D])
    out_bias = sb("bo", [P, D]) if proj else bv
    b_q = sb("b_q", [P, KC])
    b_k = sb("b_k", [P, KC])
    beta = sb("beta", [P, 1])
    stats = sb("stats", [P, TILES, 6])
    pause = sb("pause", [P, 1])
    mv = sb("mv", [P, TILES, 2])
    var = sb("var", [P, TILES])
    half = sb("half", [P, TILES])
    rstd = sb("rstd", [P, TILES])
    nbias = sb("nbias", [P, TILES])
    mx = sb("mx", [P, 2, HEADS])
    mn = sb("mn", [P, 2, HEADS])
    most = sb("most", [P, HEADS])
    rs = sb("rs", [P, HEADS])

    psT = ctx.enter_context(nc.psum_tensor(f"{name}_psT", [P, 512], F32))
    psW = [ctx.enter_context(nc.psum_tensor(f"{name}_psW{b}", [P, 512], F32)) for b in range(2)]
    psS = ctx.enter_context(nc.psum_tensor(f"{name}_psS", [P, 2, 512], F32))
    psP = ctx.enter_context(nc.psum_tensor(f"{name}_psP", [P, 2, 512], F32))
    psO = ctx.enter_context(nc.psum_tensor(f"{name}_psO", [P, 512], F32))
    psQ = [psW[0], psW[0] if proj else psT, psW[0]]
    psK = [psW[1], psO, psW[1]]
    S_all = psS[:, :, :].rearrange("p a b -> p (a b)")[:, 0:HEADS * NODES]
    P_all = psP[:, :, :].rearrange("p a b -> p (a b)")[:, 0:PAIRS * P]
    O_all = psO[:, 0:HEADS * (HD + 1)].rearrange("p (h d) -> p h d", h=HEADS)

    w_hi_set = sem("w_hi_set")
    w_lo_set = sem("w_lo_set")
    zeroed = sem("zeroed")
    consts = sem("consts")
    xl_in = sem("xl_in")
    adj_in = sem("adj_in")
    xr_in = sem("xr_in")
    xr_set = sem("xr_set")
    bias_set = None if proj else sem("bias_set")
    var_set = sem("var_set")
    rstd_set = sem("rstd_set")
    nbias_set = sem("nbias_set")
    h_set = sem("h_set")
    hT_done = sem("hT_done")
    hT_hi_set = sem("hT_hi_set")
    hT_set = sem("hT_set")
    q_done = sem("q_done")
    k_done = sem("k_done")
    q_set = sem("q_set")
    k_set = sem("k_set")
    s_done = sem("s_done")
    s_read = sem("s_read")
    mx_set = sem("mx_set")
    d_set = sem("d_set")
    e_set = sem("e_set")
    eT_done = sem("eT_done")
    eT_set = sem("eT_set")
    v_done = sem("v_done")
    v_set = sem("v_set")
    o_done = sem("o_done")
    o_set = sem("o_set")
    oT_done = sem("oT_done") if proj else None
    oT_hi_set = sem("oT_hi_set") if proj else None
    oT_set = sem("oT_set") if proj else None
    y_done = sem("y_done") if proj else None
    y_read = sem("y_read") if proj else None
    y_set = sem("y_set")
    stored = sem("stored")
    dve_step = sem("dve_step")

    def rows(ap, i):
        return ap[bass.ds(i * COLS, COLS), :].rearrange("(t p) n -> p t n", p=P)

    last = GROUPS - 1
    block = ctx.enter_context(nc.Block())

    @block.sync
    def _(sp):
        sp.dma_start(xl[:], rows(x_in, 0)).then_inc(xl_in, 16)
        load_weights(sp, raw, own_weights, shared["w_loaded"])
        n_consts = 0
        for dst, src in biases(bv, out_bias, b_q, b_k, beta):
            sp.dma_start(dst, src).then_inc(consts, 16)
            n_consts += 1
        assert n_consts == (2 if proj else 4)
        sp.dma_start(adj[:], rows(adj_rows, 0)).then_inc(adj_in, 16)
        sp.dma_start(xr[:], rows(x_in, 0)).then_inc(xr_in, 16)

        sp.wait_ge(h_set, TILES)
        sp.dma_start(xl[:], rows(x_in, 1)).then_inc(xl_in, 16)

        sp.wait_ge(w_lo_set, n_w)
        load_weights(sp, raw, next_weights, shared["w_loaded"])

        def turn(i, ahead, load_ahead=False):
            if load_ahead:
                sp.wait_ge(h_set, i * TILES + 2 * TILES)
                sp.dma_start(xl[:], rows(x_in, i + 2)).then_inc(xl_in, 16)
            for t in range(TILES):
                if t == 2 and ahead:
                    if proj:
                        sp.wait_ge(s_read, i * TILES + TILES)
                    else:
                        sp.wait_ge(bias_set, i + 1)
                    sp.dma_start(adj[:], rows(adj_rows, i + 1)).then_inc(adj_in, 16)
                sp.wait_ge(y_set, i * TILES + t + 1)
                sp.dma_start(x_out[bass.ds(i * COLS + t * P, P), :], xr[:, t, :]).then_inc(stored, 16)
            sp.wait_ge(stored, i * (16 * TILES) + 16 * TILES)
            if ahead:
                sp.dma_start(xr[:], rows(x_in, i + 1)).then_inc(xr_in, 16)

        with sp.Fori(0, last - 1) as i:
            turn(i, True, load_ahead=True)
        turn(last - 1, True)
        turn(last, False)

    @block.gpsimd
    def _(pool):
        nc.gpsimd.memset(kX[:], 0.0).then_inc(zeroed, 1)
        nc.gpsimd.memset(half[:], -0.5).then_inc(zeroed, 1)
        pool.wait_ge(zeroed, 2)

        def roots(i):
            pool.wait_ge(var_set, i + 1)
            nc.gpsimd.tensor_tensor(rstd[:], var[:], half[:], ALU.pow).then_inc(rstd_set, 1)

        roots(0)
        nc.gpsimd.memset(vX[:], 0.0).then_inc(zeroed, 1)
        pool.wait_ge(zeroed, 3)
        for b in range(2):
            nc.gpsimd.memset(vX[NODES * b:NODES * (b + 1), :, :, :, b, HD:HD + 1], 1.0).then_inc(zeroed, 1)
        pool.wait_ge(consts, 32 if proj else 64)

        def less_maximum(i, t):
            pool.wait_ge(mx_set, i * TILES + t + 1)
            if t >= 1:
                pool.wait_ge(e_set, i * TILES + t)
            nc.gpsimd.tensor_tensor(s_d[:], s_b[:, t % 2],
                                    mx[:, t % 2, :].rearrange("p (h n) -> p h n", n=1).broadcast_to([P, HEADS, NODES]),
                                    ALU.subtract).then_inc(d_set, 1)

        def residual(i, t):
            if t == 0:
                pool.wait_ge(xr_in, i * 16 + 16)
            nc.gpsimd.tensor_tensor(xr[:, t, :], xr[:, t, :], out_bias[:], ALU.add).then_inc(xr_set, 1)

        def result(i, t):
            pool.wait_ge(xr_set, i * TILES + t + 1)
            pool.wait_ge(y_read if proj else o_set, i * TILES + t + 1)
            nc.gpsimd.tensor_tensor(xr[:, t, :], xr[:, t, :], y_rows[:, t % 2, :], ALU.add).then_inc(y_set, 1)

        behind = 2 if proj else 1

        def turn(i, ahead):
            if ahead:
                roots(i + 1)
            for t in range(TILES):
                less_maximum(i, t)
                residual(i, t)
                if t >= behind:
                    result(i, t - behind)
            for t in range(TILES - behind, TILES):
                result(i, t)

        with pool.Fori(0, last) as i:
            turn(i, True)
        turn(last, False)

    @block.scalar
    def _(act):

        def weights(slots):
            for s in slots:
                act.wait_ge(shared["w_loaded"], shared["w_count"][name])
                nc.scalar.activation(w_hi[:, s], raw[:, s], ACT.Copy).then_inc(w_hi_set, 1)


        def normalise(i, tiles=range(TILES)):
            act.wait_ge(nbias_set, i + 1)
            for t in tiles:
                nc.scalar.activation(h[:, t, :], xl[:, t, :], ACT.Relu, bias=nbias[:, t:t + 1],
                                     scale=rstd[:, t:t + 1]).then_inc(h_set, 1)

        def hT_parts(i, t):
            act.wait_ge(hT_done, i * TILES + t + 1)
            nc.scalar.activation(hT_hi[:, :, t * P:(t + 1) * P], psS[:, t % 2, 0:D].rearrange("p (c n) -> p c n", c=KC),
                                 ACT.Copy).then_inc(hT_hi_set, 1)

        def keys(i, c):
            act.wait_ge(k_done, i * KC + c + 1)
            for m in range(HPC):
                part = slice(HD * m, HD * (m + 1))
                src = psK[c][part, :].rearrange("p (g n) -> p g n", g=2 * TILES)
                if proj:
                    ins = nc.scalar.activation(kX[part, c, :, m, :], src, ACT.Copy)
                else:
                    ins = nc.scalar.activation(kX[part, c, :, m, :], src, ACT.Identity, bias=b_k[part, c:c + 1])
            ins.then_inc(k_set, 1)

        def exponentials(i, t):
            act.wait_ge(d_set, i * TILES + t + 1)
            nc.scalar.activation(e_x[:], s_d[:].rearrange("p h n -> p (h n)"), ACT.Exp).then_inc(e_set, 1)

        def values(i, t):
            act.wait_ge(v_done, i * TILES + t + 1)
            if t >= 2:
                act.wait_ge(o_done, i * TILES + t - 1)
            for g in range(2):
                for b in range(2):
                    part = slice(NODES * b, NODES * (b + 1))
                    src = psW[0][NODES * g:NODES * (g + 1), 0:D].rearrange("p (a b d) -> p a b d", b=2, d=HD)[:, :, b, :]
                    ins = nc.scalar.activation(vX[part, t % 2, g, :, b, 0:HD], src, ACT.Copy)
            ins.then_inc(v_set, 1)

        def eT_copy(i, t):
            act.wait_ge(eT_done, i * TILES + t + 1)
            nc.scalar.activation(eT[:, :, :].rearrange("p a n -> p (a n)"), P_all, ACT.Copy).then_inc(eT_set, 1)

        def oT_parts(i, t):
            act.wait_ge(oT_done, i * TILES + t + 1)
            nc.scalar.activation(oT_hi[:], psT[:, 0:D].rearrange("p (c n) -> p c n", c=KC), ACT.Copy)\
              .then_inc(oT_hi_set, 1)

        if not proj:
            weights((0, 1))
        def y_copy(i, t):
            if t == 0:
                act.wait_ge(y_set, i * TILES)
            elif t >= 2:
                act.wait_ge(y_set, i * TILES + t - 1)
            act.wait_ge(y_done, i * TILES + t + 1)
            nc.scalar.activation(y_rows[:, t % 2, :], psW[1][:, 0:D], ACT.Copy).then_inc(y_read, 1)

        normalise(0)
        for t in range(TILES):
            hT_parts(0, t)
        weights(range(0 if proj else 2, n_w))
        act.wait_ge(consts, 32 if proj else 64)
        act.wait_ge(zeroed, 5)
        for c in range(KC):
            keys(0, c)
        if not proj:
            values(0, 0)

        def turn(i, ahead):
            for t in range(TILES):
                if proj and t >= 2:
                    oT_parts(i, t - 2)
                if t >= 1:
                    eT_copy(i, t - 1)
                if not proj and t == 0:
                    values(i, 1)
                if ahead and t == TILES - 1:
                    hT_parts(i + 1, 0)
                    hT_parts(i + 1, 1)
                exponentials(i, t)
                if proj and t >= 2:
                    y_copy(i, t - 2)
                if not proj and 1 <= t < TILES - 1:
                    values(i, t + 1)
                if t in (1, 2) and ahead:
                    normalise(i + 1, range(2 * (t - 1), 2 * t))
            if ahead and not proj:
                hT_parts(i + 1, 2)
                hT_parts(i + 1, 3)
            eT_copy(i, TILES - 1)
            if proj:
                oT_parts(i, TILES - 2)
            if ahead:
                if proj:
                    hT_parts(i + 1, 2)
                    hT_parts(i + 1, 3)
                if proj:
                    y_copy(i, TILES - 2)
                    oT_parts(i, TILES - 1)
                for c in range(KC):
                    keys(i + 1, c)
                    if proj and c == 0:
                        y_copy(i, TILES - 1)
                if not proj:
                    values(i + 1, 0)
            elif proj:
                y_copy(i, TILES - 2)
                oT_parts(i, TILES - 1)
                y_copy(i, TILES - 1)

        with act.Fori(0, last) as i:
            turn(i, True)
        turn(last, False)

    @block.vector
    def _(dve):
        step = Steps(dve, dve_step, 0)

        def weights(slots):
            for s in slots:
                dve.wait_ge(w_hi_set, s + 1)
                nc.vector.tensor_tensor(w_lo[:, s], raw[:, s], w_hi[:, s].bitcast(F32), ALU.subtract)\
                  .then_inc(w_lo_set, 1)


        def statistics(i):
            dve.wait_ge(xl_in, i * 16 + 16)
            for t in range(TILES):
                ins = nc.vector.bn_stats(stats[:, t, :], xl[:, t, :])
            step.done(ins)
            nc.vector.memset(pause[:], 0.0)
            for t in range(TILES):
                ins = nc.vector.bn_aggr(mv[:, t, :], stats[:, t, :])
            step.done(ins)
            nc.vector.tensor_scalar(var[:], mv[:, :, 1], LN_EPS, None, ALU.add).then_inc(var_set, 1)

        def shifts(i):
            dve.wait_ge(rstd_set, i + 1)
            nc.vector.scalar_tensor_tensor(nbias[:], mv[:, :, 0], -1.0, rstd[:], ALU.mult, ALU.mult)\
              .then_inc(nbias_set, 1)

        def hT_parts(i, t):
            dve.wait_ge(hT_hi_set, i * TILES + t + 1)
            cols = slice(t * P, (t + 1) * P)
            nc.vector.tensor_tensor(hT_lo[:, :, cols], psS[:, t % 2, 0:D].rearrange("p (c n) -> p c n", c=KC),
                                    hT_hi[:, :, cols].bitcast(F32), ALU.subtract).then_inc(hT_set, 1)

        def queries(i, c):
            dve.wait_ge(q_done, i * KC + c + 1)
            if proj:
                nc.vector.tensor_scalar(qT[:, c, :], psQ[c][:], scale, None, ALU.mult).then_inc(q_set, 1)
            else:
                nc.vector.tensor_scalar(qT[:, c, :], psQ[c][:], b_q[:, c:c + 1], scale, ALU.add, ALU.mult)\
                  .then_inc(q_set, 1)

        def score_bias(i):
            dve.wait_ge(adj_in, i * 16 + 16)
            step.done(nc.vector.tensor_scalar(masked[:], adj[:], 0.0, -BIG, ALU.is_le, ALU.mult))
            nc.vector.scalar_tensor_tensor(bias_qk[:], adj[:], beta[:], masked[:], ALU.mult, ALU.add)\
              .then_inc(bias_set, 1)

        def add_bias(i, t):
            if t == 0:
                if proj:
                    dve.wait_ge(adj_in, i * 16 + 16)
                else:
                    dve.wait_ge(bias_set, i + 1)
            dve.wait_ge(s_done, i * TILES + t + 1)
            if t >= 2:
                dve.wait_ge(d_set, i * TILES + t - 1)
            if proj and t >= 1:
                step.catch_up()
            nc.vector.tensor_tensor(s_b[:, t % 2], S_all.rearrange("p (h n) -> p h n", h=HEADS),
                                    bias_qk[:, t:t + 1, :].broadcast_to([P, HEADS, NODES]), ALU.add)\
              .then_inc(s_read, 1)

        def maximum(i, t):
            dve.wait_ge(s_read, i * TILES + t + 1)
            nc.vector.tensor_reduce(mx[:, t % 2, :], s_b[:, t % 2], axis=AX.X, op=ALU.max).then_inc(mx_set, 1)

        def least(i, t):
            step.mark(nc.vector.tensor_reduce(mn[:, t % 2, :], s_b[:, t % 2], axis=AX.X, op=ALU.min))

        def values(i, t):
            dve.wait_ge(v_done, i * TILES + t + 1)
            if t >= 2:
                dve.wait_ge(o_done, i * TILES + t - 1)
            for g in range(2):
                for b in range(2):
                    part = slice(NODES * b, NODES * (b + 1))
                    src = psW[0][NODES * g:NODES * (g + 1), 0:D].rearrange("p (a b d) -> p a b d", b=2, d=HD)[:, :, b, :]
                    bias = bv[part, :].rearrange("p (a b d) -> p a b d", b=2, d=HD)[:, :, b, :]
                    ins = nc.vector.tensor_tensor(vX[part, t % 2, g, :, b, 0:HD], src, bias, ALU.add)
            ins.then_inc(v_set, 1)

        def row_output(i, t):
            dve.wait_ge(o_done, i * TILES + t + 1)
            if not proj and t >= 2:
                dve.wait_ge(y_set, i * TILES + t - 1)
            if proj:
                dve.wait_ge(mx_set, i * TILES + t + 1)
                nc.vector.scalar_tensor_tensor(most[:], mn[:, t % 2, :], -1.0, mx[:, t % 2, :], ALU.mult, ALU.max)
            step.done(nc.vector.reciprocal(rs[:], O_all[:, :, HD]))
            if proj:
                step.done(nc.vector.scalar_tensor_tensor(rs[:], most[:], 0.0, rs[:], ALU.not_equal, ALU.mult))
            ins = nc.vector.tensor_tensor(o_rows[:, t % 2, :].rearrange("p (h d) -> p h d", h=HEADS), O_all[:, :, 0:HD],
                                          rs[:, :].rearrange("p (h n) -> p h n", n=1).broadcast_to([P, HEADS, HD]),
                                          ALU.mult)
            ins.then_inc(o_set, 1)

        def oT_parts(i, t):
            dve.wait_ge(oT_hi_set, i * TILES + t + 1)
            nc.vector.tensor_tensor(oT_lo[:], psT[:, 0:D].rearrange("p (c n) -> p c n", c=KC),
                                    oT_hi[:].bitcast(F32), ALU.subtract).then_inc(oT_set, 1)

        statistics(0)
        if not proj:
            weights((0,))
        shifts(0)
        for t in range(TILES):
            hT_parts(0, t)
        weights(range(0 if proj else 1, 2))
        dve.wait_ge(consts, 32 if proj else 64)
        dve.wait_ge(zeroed, 5)
        for c in range(KC):
            queries(0, c)
            if c + 2 < n_w:
                weights((c + 2,))
        if not proj:
            score_bias(0)
        before = step.n
        step.per = 2 + TILES * 3 if proj else 3 + TILES

        def turn(i, ahead):
            step.turn(i, before)
            if ahead:
                statistics(i + 1)
            if proj:
                values(i, 0)
            for t in range(TILES):
                add_bias(i, t)
                if proj and t >= 2:
                    oT_parts(i, t - 2)
                maximum(i, t)
                if proj and t == 0:
                    values(i, 1)
                if proj:
                    least(i, t)
                if ahead and t == TILES - 1:
                    hT_parts(i + 1, 0)
                    hT_parts(i + 1, 1)
                if t >= 1:
                    row_output(i, t - 1)
                if proj and 1 <= t < TILES - 1:
                    values(i, t + 1)
                if t == 0 and ahead:
                    shifts(i + 1)
            if proj:
                oT_parts(i, TILES - 2)
            if ahead:
                hT_parts(i + 1, 2)
                hT_parts(i + 1, 3)
                if not proj:
                    score_bias(i + 1)
            row_output(i, TILES - 1)
            if ahead:
                queries(i + 1, 0)
            if proj:
                oT_parts(i, TILES - 1)
            if ahead:
                queries(i + 1, 1)
            if ahead:
                queries(i + 1, 2)

        with dve.Fori(0, last) as i:
            turn(i, True)
            step.ended()
        turn(last, False)

    @block.tensor
    def _(pe):
        pe.wait_ge(shared["ident_set"], 2)
        Q, K, V, O = range(4)

        def w_cols(s, cols):
            return tuple((lambda c, w=w: w[:, s, c, cols]) for w in (w_hi, w_lo))

        def h_cols(cols):
            return tuple((lambda c, x=x: x[:, c, cols]) for x in (hT_hi, hT_lo))

        def transposes(i, t):
            pe.wait_ge(h_set, i * TILES + t + 1)
            if t >= 2:
                pe.wait_ge(hT_set, i * TILES + t - 1)
            for c in range(KC):
                ins = nc.tensor.transpose(psS[:, t % 2, c * P:(c + 1) * P], h[:, t, c * P:(c + 1) * P], ident[:])
            ins.then_inc(hT_done, 1)

        def queries(i, c):
            if proj and c == 1 or c == 2:
                pe.wait_ge(q_set, i * KC + (c if proj else 1))
            split_matmul(nc, psQ[c][:], w_cols(Q, slice(c * P, (c + 1) * P)), h_cols(slice(0, COLS))).then_inc(q_done, 1)

        def keys(i, c):
            split_matmul(nc, psK[c][:], w_cols(K, slice(c * P, (c + 1) * P)), h_cols(slice(0, COLS))).then_inc(k_done, 1)

        def scores(i, t):
            if t == 0:
                pe.wait_ge(q_set, i * KC + KC)
                pe.wait_ge(hT_set, i * TILES + TILES)
            else:
                pe.wait_ge(s_read, i * TILES + t)
            for c in range(KC):
                if t == 0:
                    pe.wait_ge(k_set, i * KC + c + 1)
                for g in range(2):
                    lo = t * P + g * NODES
                    ins = nc.tensor.matmul(S_all[NODES * g:NODES * (g + 1), c * HPC * NODES:(c + 1) * HPC * NODES],
                                           qT[:, c, lo:lo + NODES], kX[:, c, 2 * t + g].rearrange("p h n -> p (h n)"),
                                           start=True, stop=True)
            ins.then_inc(s_done, 1)

        def values(i, t):
            if t == 0:
                pe.wait_ge(q_set, i * KC + KC)
            else:
                pe.wait_ge(v_set, i * TILES + t)
            split_matmul(nc, psW[0][:, 0:D], h_cols(slice(t * P, (t + 1) * P)), w_cols(V, slice(0, D))).then_inc(v_done, 1)

        def exp_transposes(i, t):
            pe.wait_ge(e_set, i * TILES + t + 1)
            for a in range(PAIRS):
                ins = nc.tensor.transpose(P_all[:, a * P:(a + 1) * P], e_x[:, a * P:(a + 1) * P], ident[:])
            ins.then_inc(eT_done, 1)

        def weigh(i, t):
            pe.wait_ge(eT_set, i * TILES + t + 1)
            pe.wait_ge(v_set, i * TILES + t + 1)
            if not proj and t >= 1:
                pe.wait_ge(o_set, i * TILES + t)
            for a in range(PAIRS):
                for g in range(2):
                    ins = nc.tensor.matmul(psO[NODES * g:NODES * (g + 1), a * 2 * (HD + 1):(a + 1) * 2 * (HD + 1)],
                                           eT[:, a, NODES * g:NODES * (g + 1)],
                                           vX[:, t % 2, g, a].rearrange("p b d -> p (b d)"), start=True, stop=True)
            ins.then_inc(o_done, 1)

        def out_transposes(i, t):
            pe.wait_ge(o_set, i * TILES + t + 1)
            for c in range(KC):
                ins = nc.tensor.transpose(psT[:, c * P:(c + 1) * P], o_rows[:, t % 2, c * P:(c + 1) * P], ident[:])
            ins.then_inc(oT_done, 1)

        def project(i, t, behind_keys=False):
            pe.wait_ge(oT_set, i * TILES + t + 1)
            if behind_keys:
                pe.wait_ge(k_set, i * KC + KC + 1)
            elif t >= 1:
                pe.wait_ge(y_read, i * TILES + t)
            oT = tuple((lambda c, x=x: x[:, c, :]) for x in (oT_hi, oT_lo))
            split_matmul(nc, psW[1][:, 0:D], oT, w_cols(O, slice(0, D))).then_inc(y_done, 1)

        def queries_and_keys(i, before_last=None):
            if not before_last:
                pe.wait_ge(w_lo_set, Q + 1)
            queries(i, 0)
            if before_last and proj:
                out_transposes(before_last[0], TILES - 1)
                pe.wait_ge(y_read, before_last[0] * TILES + TILES - 1)
            if not before_last:
                pe.wait_ge(w_lo_set, K + 1)
            keys(i, 0)
            queries(i, 1)
            if before_last and proj:
                project(*before_last, behind_keys=True)
            queries(i, 2)
            if before_last and proj:
                pe.wait_ge(y_read, before_last[0] * TILES + TILES)
            if before_last:
                pe.wait_ge(o_set, before_last[0] * TILES + TILES)
            keys(i, 1)
            pe.wait_ge(k_set, i * KC + 1)
            keys(i, 2)
            if not before_last:
                pe.wait_ge(w_lo_set, n_w)
            values(i, 0)

        for t in range(TILES):
            transposes(0, t)
        pe.wait_ge(hT_set, TILES)
        queries_and_keys(0)

        def turn(i, ahead):
            for t in range(TILES):
                scores(i, t)
                if proj and t >= 2:
                    out_transposes(i, t - 2)
                if t < 2:
                    values(i, t + 1)
                if t >= 1:
                    exp_transposes(i, t - 1)
                if t == 2:
                    values(i, t + 1)
                if ahead and t == TILES - 1:
                    pe.wait_ge(s_read, i * TILES + TILES)
                    transposes(i + 1, 0)
                    transposes(i + 1, 1)
                if proj and t >= 2:
                    project(i, t - 2)
                if t >= 1:
                    weigh(i, t - 1)
            if ahead and not proj:
                transposes(i + 1, 2)
                transposes(i + 1, 3)
            exp_transposes(i, TILES - 1)
            if proj:
                out_transposes(i, TILES - 2)
            if ahead and proj:
                transposes(i + 1, 2)
                transposes(i + 1, 3)
            weigh(i, TILES - 1)
            if proj:
                project(i, TILES - 2)
            if ahead:
                pe.wait_ge(v_set, i * TILES + TILES)
                pe.wait_ge(hT_set, i * TILES + 2 * TILES)
                queries_and_keys(i + 1, (i, TILES - 1))
            elif proj:
                out_transposes(i, TILES - 1)
                project(i, TILES - 1)

        with pe.Fori(0, last) as i:
            turn(i, True)
        turn(last, False)


def bilinear_phase(nc, ctx, shared, x_in, adj, x_out, a, next_weights):
    w_hi, w_lo, raw, ident = shared["w_hi"], shared["w_lo"], shared["raw"], shared["ident"]
    n_w = 6
    eps, var_scale = 1e-3, float(D) / (D - 1)

    def sb(n, shape, dt=F32):
        return ctx.enter_context(nc.sbuf_tensor(f"l1_{n}", shape, dt))

    def ps(n):
        return ctx.enter_context(nc.psum_tensor(f"l1_{n}", [P, 512], F32))

    def sem(n):
        return ctx.enter_context(nc.semaphore(f"l1_{n}"))

    xl = [sb(f"xl{g}", [P, TILES, D]) for g in range(2)]
    xr = sb("xr", [P, TILES, D])
    hT = [(sb(f"hT{k}_hi", [P, KC, COLS], F32R), sb(f"hT{k}_lo", [P, KC, COLS], F32R)) for k in range(4)]
    hT_whole = [sb(f"hT_whole{g}", [P, KC, COLS]) for g in range(2)]
    m = sb("m", [P, 2, KC, COLS])
    adj_bd = [sb(f"adj_bd{g}", [P, TILES, P]) for g in range(2)]
    adj_rows = [sb(f"adj_rows{g}", [P, TILES, NODES]) for g in range(2)]
    adjT = sb("adjT", [P, TILES, NODES])
    masks = [sb(f"masks{g}", [P, TILES, 2, NODES]) for g in range(2)]
    tri = sb("tri", [P, 2, NODES])
    u_parts = sb("u_parts", [P, 2, NODES])
    u_sum = sb("u_sum", [P, NODES])
    e_u = sb("e_u", [P, NODES])
    delta = sb("delta", [P, 2, P])
    dT = sb("dT", [P, 2, P])
    lin = sb("lin", [P, 2, D + 1])
    act_rows = sb("act_rows", [P, 2, D])
    b_lin, ln_a, ln_b = (sb(n, [P, 2, D]) for n in ("b_lin", "ln_a", "ln_b"))
    half = sb("half", [P, 2])
    stats = sb("stats", [P, TILES, 6])
    pause = sb("pause", [P, 1])
    mv = sb("mv", [P, TILES, 2])
    var = sb("var", [P, TILES])
    rstd = sb("rstd", [P, TILES])
    nbias = sb("nbias", [P, TILES])
    c_sum, c_r, c_var, c_root, c_inv, c_scale, c_nb = (sb(n, [P, TILES]) for n in (
        "c_sum", "c_r", "c_var", "c_root", "c_inv", "c_scale", "c_nb"))
    c_stats = sb("c_stats", [P, TILES, 6])
    c_mv = sb("c_mv", [P, TILES, 2])

    psU, psX = ps("psU"), ps("psX")
    psW, psC, psT = ([ps(f"{n}{b}") for b in range(2)] for n in ("psW", "psC", "psT"))

    w_hi_set = sem("w_hi_set")
    w_lo_set = sem("w_lo_set")
    zeroed = sem("zeroed")
    consts = sem("consts")
    xl_in = [sem(f"xl_in{g}") for g in range(2)]
    adj_in = [sem(f"adj_in{g}") for g in range(2)]
    xr_in = sem("xr_in")
    var_set = sem("var_set")
    rstd_set = sem("rstd_set")
    nbias_set = sem("nbias_set")
    h_set = sem("h_set")
    hT_done = sem("hT_done")
    hT_hi_set = sem("hT_hi_set")
    hT_set = sem("hT_set")
    m_done = sem("m_done")
    m_set = sem("m_set")
    adjT_done = sem("adjT_done")
    adjT_set = sem("adjT_set")
    masks_set = sem("masks_set")
    u_done = sem("u_done")
    u_set = sem("u_set")
    e_set = sem("e_set")
    d_set = sem("d_set")
    dT_done = sem("dT_done")
    dT_set = sem("dT_set")
    lin_done = sem("lin_done")
    lin_set = sem("lin_set")
    c_done = sem("c_done")
    c_var_set = sem("c_var_set")
    c_root_set = sem("c_root_set")
    c_ln_set = sem("c_ln_set")
    rows_set = sem("rows_set")
    affine_set = sem("affine_set")
    y_set = sem("y_set")
    stored = sem("stored")
    dve_step = sem("dve_step")
    pool_step = sem("pool_step")

    def rows(ap, q):
        return ap[bass.ds(q * COLS, COLS), :].rearrange("(t p) n -> p t n", p=P)

    turns = GROUPS // 2
    last = turns - 1
    block = ctx.enter_context(nc.Block())

    @block.sync
    def _(sp):
        for g in range(2):
            sp.dma_start(xl[g][:], rows(x_in, g)).then_inc(xl_in[g], 16)
        for dst, name in ((b_lin, "L1_gnn_b_lin"), (ln_a, "L1_gnn_ln_a"), (ln_b, "L1_gnn_ln_b")):
            sp.dma_start(dst[:], a[name].partition_broadcast(P)).then_inc(consts, 16)

        def load_adj(q, group):
            graphs = adj[bass.ds(q * 2 * TILES, 2 * TILES), :, :].rearrange("(t g) i j -> g i t j", g=2)
            for g in range(2):
                sp.dma_start(adj_bd[group][NODES * g:NODES * (g + 1), :, NODES * g:NODES * (g + 1)], graphs[g])\
                  .then_inc(adj_in[group], 16)
            sp.dma_start(adj_rows[group][:], rows(adj.rearrange("b i j -> (b i) j"), q)).then_inc(adj_in[group], 16)

        def store(i, k):
            for t in range(TILES):
                sp.wait_ge(y_set, (2 * i + k - 2) * TILES + t + 1)
                sp.dma_start(x_out[bass.ds((2 * i + k - 2) * COLS + t * P, P), :], xr[:, t, :]).then_inc(stored, 16)
            sp.wait_ge(stored, (2 * i + k - 1) * (16 * TILES))

        sp.dma_start(xr[:], rows(x_in, 0)).then_inc(xr_in, 16)
        sp.wait_ge(zeroed, 2)
        load_adj(0, 0)
        load_adj(1, 1)
        sp.wait_ge(w_lo_set, n_w)
        load_weights(sp, raw, next_weights, shared["w_loaded"])

        def turn(i, ahead):
            if ahead:
                sp.wait_ge(hT_done, (4 * i + 2) * TILES)
                for g in range(2):
                    sp.dma_start(xl[g][:], rows(x_in, 2 * i + 2 + g)).then_inc(xl_in[g], 16)
                sp.wait_ge(d_set, (4 * i + 3) * TILES)
                load_adj(2 * i + 2, 0)
            store(i, 2)
            sp.dma_start(xr[:], rows(x_in, 2 * i + 1)).then_inc(xr_in, 16)
            if ahead:
                sp.wait_ge(d_set, (4 * i + 4) * TILES)
                load_adj(2 * i + 3, 1)
            store(i, 3)
            if ahead:
                sp.dma_start(xr[:], rows(x_in, 2 * i + 2)).then_inc(xr_in, 16)

        with sp.Fori(0, last) as i:
            turn(i, True)
        turn(last, False)

    @block.gpsimd
    def _(pool):
        step = Steps(pool, pool_step, 4 * TILES)
        for g in range(2):
            nc.gpsimd.memset(adj_bd[g][:], 0.0).then_inc(zeroed, 1)
        nc.gpsimd.memset(half[:, 0:1], -0.5).then_inc(zeroed, 1)
        nc.gpsimd.memset(half[:, 1:2], 0.5).then_inc(zeroed, 1)
        nc.gpsimd.memset(lin[:, :, D:D + 1], 1.0).then_inc(zeroed, 1)
        nc.gpsimd.memset(delta[:], 0.0).then_inc(zeroed, 1)
        nc.gpsimd.memset(tri[:], 1.0).then_inc(zeroed, 1)
        pool.wait_ge(zeroed, 7)
        for s, (sign, compare) in enumerate(((1, ALU.is_ge), (-1, ALU.is_gt))):
            for g in range(2):
                part = tri[NODES * g:NODES * (g + 1), s, :]
                nc.gpsimd.affine_select(out=part, in_=part, compare_op=compare, fill=0.0, base=0,
                                        pattern=[[sign, NODES]], channel_multiplier=-sign).then_inc(zeroed, 1)
        pool.wait_ge(zeroed, 11)

        def roots(q):
            pool.wait_ge(var_set, q + 1)
            nc.gpsimd.tensor_tensor(rstd[:], var[:], half[:, 0:1].broadcast_to([P, TILES]), ALU.pow).then_inc(rstd_set, 1)

        def make_masks(q, g):
            pool.wait_ge(adjT_set, q + 1)
            for side, source in enumerate((adj_rows[g], adjT)):
                nc.gpsimd.tensor_tensor(masks[g][:, :, side, :], source[:],
                                        tri[:, side:side + 1, :].broadcast_to([P, TILES, NODES]), ALU.mult)\
                  .then_inc(masks_set, 1)

        def root(i, k, t):
            pool.wait_ge(c_var_set, (4 * i + k) * TILES + t + 1)
            nc.gpsimd.tensor_tensor(c_root[:, t:t + 1], c_var[:, t:t + 1], half[:, 1:2], ALU.pow).then_inc(c_root_set, 1)

        def affine(i, k, t):
            pool.wait_ge(rows_set, (4 * i + k) * TILES + t + 1)
            row = act_rows[:, t % 2, :]
            step.done(nc.gpsimd.tensor_tensor(row, row, ln_a[:, k // 2, :], ALU.mult))
            nc.gpsimd.tensor_tensor(row, row, ln_b[:, k // 2, :], ALU.add).then_inc(affine_set, 1)

        def unit(i, k, ahead):
            for t in range(TILES):
                if t >= 1:
                    root(i, k, t - 1)
                if t >= 2:
                    affine(i, k, t - 2)
            affine(i, k, 2)
            root(i, k, 3)
            if ahead and k in (1, 2):
                roots(2 * i + k + 1)
            affine(i, k, 3)
            if k == 0:
                make_masks(2 * i + 1, 1)
            if k == 3 and ahead:
                make_masks(2 * i + 2, 0)

        roots(0)
        roots(1)
        pool.wait_ge(consts, 48)
        make_masks(0, 0)

        def turn(i, ahead):
            step.turn(i, 0)
            for k in range(4):
                unit(i, k, ahead)

        with pool.Fori(0, last) as i:
            turn(i, True)
            step.ended()
        turn(last, False)

    @block.scalar
    def _(act):
        act.wait_ge(shared["w_loaded"], shared["w_count"]["l1"])

        def weights(slots):
            for s in slots:
                nc.scalar.activation(w_hi[:, s], raw[:, s], ACT.Copy).then_inc(w_hi_set, 1)


        def normalise(q, tiles=range(TILES)):
            act.wait_ge(nbias_set, 2 * q[0] + q[1] + 1)
            for t in tiles:
                nc.scalar.activation(xl[q[1]][:, t, :], xl[q[1]][:, t, :], ACT.Relu, bias=nbias[:, t:t + 1],
                                     scale=rstd[:, t:t + 1]).then_inc(h_set, 1)

        def hT_part(index, k, t):
            act.wait_ge(hT_done, index + 1)
            nc.scalar.activation(hT_whole[k % 2][:, :, t * P:(t + 1) * P],
                                 psT[t % 2][:, 0:D].rearrange("p (c n) -> p c n", c=KC), ACT.Relu)
            nc.scalar.activation(hT[k][0][:, :, t * P:(t + 1) * P],
                                 psT[t % 2][:, 0:D].rearrange("p (c n) -> p c n", c=KC), ACT.Relu).then_inc(hT_hi_set, 1)

        def m_part(i, k, j):
            act.wait_ge(m_done, (4 * i + k) * 2 * KC + j + 1)
            nc.scalar.activation(m[:, j // KC, j % KC, :], psW[j % 2][:], ACT.Copy).then_inc(m_set, 1)

        def exponential(i, k, t):
            act.wait_ge(u_set, (4 * i + k) * TILES + t + 1)
            nc.scalar.activation(e_u[:], u_sum[:], ACT.Exp, scale=float(D) ** -0.5).then_inc(e_set, 1)

        def norm_rows(i, k, t):
            act.wait_ge(c_ln_set, (4 * i + k) * TILES + t + 1)
            nc.scalar.activation(act_rows[:, t % 2, :], psC[t % 2][:, 0:D], ACT.Identity, bias=c_nb[:, t:t + 1],
                                 scale=c_scale[:, t:t + 1]).then_inc(rows_set, 1)

        def dT_copy(i, k, t):
            act.wait_ge(dT_done, (4 * i + k) * TILES + t + 1)
            nc.scalar.activation(dT[:, t % 2, :], psX[:, (t % 2) * P:(t % 2 + 1) * P], ACT.Copy).then_inc(dT_set, 1)

        def adjT_copy(q):
            act.wait_ge(adjT_done, q + 1)
            if not (isinstance(q, int) and q == 0):
                act.wait_ge(masks_set, 2 * q)
            for b in range(2):
                part = slice(NODES * b, NODES * (b + 1))
                ins = nc.scalar.activation(adjT[part], psX[part, :].rearrange("p (t n) -> p t n", t=TILES)[:, :, part],
                                           ACT.Copy)
            ins.then_inc(adjT_set, 1)

        def products(i, k, tail):
            def left(f, t):
                if tail:
                    f(*tail, t)

            def left_T(t):
                if tail and tail[1] < 2:
                    hT_part(2 * TILES + (4 * tail[0] + tail[1]) * TILES + t, tail[1] + 2, t)

            m_part(i, k, 0)
            left(dT_copy, 3)
            left_T(0)
            left(norm_rows, 2)
            m_part(i, k, 1)
            m_part(i, k, 2)
            left_T(1)
            m_part(i, k, 3)
            left(norm_rows, 3)
            left_T(2)
            m_part(i, k, 4)
            m_part(i, k, 5)
            left_T(3)

        def unit(i, k, ahead):
            for t in range(TILES):
                if t >= 1:
                    dT_copy(i, k, t - 1)
                exponential(i, k, t)
                if t >= 2:
                    norm_rows(i, k, t - 2)
                if k >= 2 and ahead:
                    hT_part(2 * TILES + (4 * i + k) * TILES + t, k - 2, t)
                    if t < TILES - 1:
                        normalise((i + 1, k - 2), (t + 1,))
            if k == 0:
                adjT_copy(2 * i + 1)
            if k == 3 and ahead:
                adjT_copy(2 * i + 2)
            if k < 3:
                products(i, k + 1, (i, k))
                if ahead and k in (1, 2):
                    normalise((i + 1, k - 1), (0,))
            elif ahead:
                products(i + 1, 0, (i, 3))
            else:
                norm_rows(i, k, 2)
                dT_copy(i, k, 3)
                norm_rows(i, k, 3)

        weights((0, 1, 2))
        normalise((0, 0))
        for t in range(TILES):
            hT_part(t, 0, t)
        adjT_copy(0)
        for j in range(2 * KC):
            m_part(0, 0, j)
            if j < TILES:
                normalise((0, 1), (j,))
            if 1 <= j <= TILES:
                hT_part(TILES + j - 1, 1, j - 1)
            if j >= KC:
                weights((j,))

        def turn(i, ahead):
            for k in range(4):
                unit(i, k, ahead)

        with act.Fori(0, last) as i:
            turn(i, True)
        turn(last, False)

    @block.vector
    def _(dve):
        step = Steps(dve, dve_step, 0)

        def weights(slots):
            for s in slots:
                dve.wait_ge(w_hi_set, s + 1)
                nc.vector.tensor_tensor(w_lo[:, s], raw[:, s], w_hi[:, s].bitcast(F32), ALU.subtract)\
                  .then_inc(w_lo_set, 1)


        def statistics(q, tiles=range(TILES)):
            if tiles[0] == 0:
                dve.wait_ge(xl_in[q[1]], q[0] * 16 + 16)
            for t in tiles:
                ins = nc.vector.bn_stats(stats[:, t, :], xl[q[1]][:, t, :])
            if tiles[-1] == TILES - 1:
                step.mark(ins)

        def variances():
            step.catch_up()
            nc.vector.memset(pause[:], 0.0)
            for t in range(TILES):
                ins = nc.vector.bn_aggr(mv[:, t, :], stats[:, t, :])
            step.done(ins)
            nc.vector.tensor_scalar(var[:], mv[:, :, 1], LN_EPS, None, ALU.add).then_inc(var_set, 1)

        def shifts(q):
            dve.wait_ge(rstd_set, 2 * q[0] + q[1] + 1)
            nc.vector.scalar_tensor_tensor(nbias[:], mv[:, :, 0], -1.0, rstd[:], ALU.mult, ALU.mult)\
              .then_inc(nbias_set, 1)

        def hT_part(index, k, t):
            dve.wait_ge(hT_hi_set, index + 1)
            hi, lo = (x[:, :, t * P:(t + 1) * P] for x in hT[k])
            nc.vector.scalar_tensor_tensor(lo, psT[t % 2][:, 0:D].rearrange("p (c n) -> p c n", c=KC), 0.0,
                                           hi.bitcast(F32), ALU.max, ALU.subtract).then_inc(hT_set, 1)

        def mask_u(i, k, t):
            if t == 0:
                dve.wait_ge(masks_set, 2 * (2 * i + k % 2 + 1))
            dve.wait_ge(u_done, (4 * i + k) * TILES + t + 1)
            step.done(nc.vector.tensor_tensor(u_parts[:], psU[:, 0:P].rearrange("p (s n) -> p s n", s=2),
                                              masks[k % 2][:, t], ALU.mult))
            nc.vector.tensor_tensor(u_sum[:], u_parts[:, 0, :], u_parts[:, 1, :], ALU.add).then_inc(u_set, 1)

        def lin_copy(i, k, t):
            dve.wait_ge(lin_done, (4 * i + k) * TILES + t + 1)
            nc.vector.tensor_tensor(lin[:, t % 2, 0:D], psW[t % 2][:, 0:D], b_lin[:, k // 2, :], ALU.add)\
              .then_inc(lin_set, 1)

        def weigh_adj(i, k, t):
            dve.wait_ge(e_set, (4 * i + k) * TILES + t + 1)
            for g in range(2):
                part = slice(NODES * g, NODES * (g + 1))
                ins = nc.vector.tensor_tensor(delta[part, t % 2, part], e_u[part], adj_rows[k % 2][part, t, :],
                                              ALU.mult)
            ins.then_inc(d_set, 1)

        def context_statistics(i, k, t):
            dve.wait_ge(c_done, (4 * i + k) * TILES + t + 1)
            one = slice(t, t + 1)
            step.mark(nc.vector.tensor_scalar(c_sum[:, one], psC[t % 2][:, D:D + 1], 1e-10, None, ALU.add))
            step.done(nc.vector.bn_stats(c_stats[:, t, :], psC[t % 2][:, 0:D]))
            step.mark(nc.vector.reciprocal(c_r[:, one], c_sum[:, one]))
            step.done(nc.vector.bn_aggr(c_mv[:, t, :], c_stats[:, t, :]))
            nc.vector.tensor_scalar(c_var[:, one], c_mv[:, t, 1:2], c_r[:, one], c_r[:, one], ALU.mult, ALU.mult)\
              .then_inc(c_var_set, 1)

        def context_norm(i, k, t):
            dve.wait_ge(c_root_set, (4 * i + k) * TILES + t + 1)
            one = slice(t, t + 1)
            step.done(nc.vector.tensor_scalar(c_inv[:, one], c_root[:, one], var_scale ** 0.5, eps, ALU.mult, ALU.add))
            step.done(nc.vector.reciprocal(c_inv[:, one], c_inv[:, one]))
            step.done(nc.vector.tensor_tensor(c_scale[:, one], c_inv[:, one], c_r[:, one], ALU.mult))
            nc.vector.scalar_tensor_tensor(c_nb[:, one], c_mv[:, t, 0:1], -1.0, c_scale[:, one], ALU.mult, ALU.mult)\
              .then_inc(c_ln_set, 1)

        def result(i, k, t):
            if t == 0:
                dve.wait_ge(xr_in, (2 * i + k - 1) * 16)
            dve.wait_ge(affine_set, (4 * i + k) * TILES + t + 1)
            nc.vector.scalar_tensor_tensor(xr[:, t, :], act_rows[:, t % 2, :], 0.0, xr[:, t, :], ALU.max, ALU.add)\
              .then_inc(y_set, 1)

        def products(i, k, tail, q):
            def left(f, t):
                if tail:
                    f(*tail, t)

            def left_end(t):
                if tail and tail[1] < 2:
                    hT_part(2 * TILES + (4 * tail[0] + tail[1]) * TILES + t, tail[1] + 2, t)
                elif tail:
                    result(*tail, t)

            left(context_norm, 2)
            if tail and tail[1] < 2:
                left_end(0)
            if q is not None:
                statistics(q, (3,))
            left(context_statistics, 3)
            left_end(1)
            left(context_norm, 3)
            if q is not None:
                variances()
            left_end(2)
            if q is not None:
                shifts(q)
            left_end(3)

        def unit(i, k, ahead):
            for t in range(TILES):
                if t == 0:
                    lin_copy(i, k, 0)
                mask_u(i, k, t)
                if t >= 2:
                    context_norm(i, k, t - 2)
                weigh_adj(i, k, t)
                if t >= 1:
                    context_statistics(i, k, t - 1)
                if t < TILES - 1:
                    lin_copy(i, k, t + 1)
                if k >= 2 and ahead:
                    hT_part(2 * TILES + (4 * i + k) * TILES + t, k - 2, t)
                if k >= 2 and t == 3:
                    result(i, k, 0)
                if ahead and k in (1, 2) and t >= 1:
                    statistics((i + 1, k - 1), (t - 1,))
            if k < 3:
                products(i, k + 1, (i, k), (i + 1, k - 1) if ahead and k in (1, 2) else None)
            elif ahead:
                products(i + 1, 0, (i, 3), None)
            else:
                context_norm(i, k, 2)
                context_statistics(i, k, 3)
                result(i, k, 1)
                context_norm(i, k, 3)
                result(i, k, 2)
                result(i, k, 3)

        statistics((0, 0))
        variances()
        weights((0,))
        shifts((0, 0))
        statistics((0, 1))
        for t in range(TILES):
            hT_part(t, 0, t)
        variances()
        dve.wait_ge(consts, 48)
        dve.wait_ge(zeroed, 11)
        shifts((0, 1))
        weights((1,))
        for j in range(2 * KC):
            if 1 <= j <= TILES:
                hT_part(TILES + j - 1, 1, j - 1)
            if j == 0 or j >= KC:
                weights((max(2, j),))
        before = step.n
        step.per = 4 * TILES * 8 + 2 * 2

        def turn(i, ahead):
            step.turn(i, before)
            for k in range(4):
                unit(i, k, ahead)

        with dve.Fori(0, last) as i:
            turn(i, True)
            step.ended()
        turn(last, False)

    @block.tensor
    def _(pe):
        pe.wait_ge(shared["ident_set"], 2)
        LEFT, RIGHT, LIN = range(3)

        def w_cols(layer, s, cols):
            return tuple((lambda c, w=w: w[:, 3 * layer + s, c, cols]) for w in (w_hi, w_lo))

        def h_cols(k, t=None):
            cols = slice(0, COLS) if t is None else slice(t * P, (t + 1) * P)
            return tuple((lambda c, x=x: x[:, c, cols]) for x in hT[k])

        def transposes(index, src, t):
            for c in range(KC):
                ins = nc.tensor.transpose(psT[t % 2][:, c * P:(c + 1) * P], src[:, c * P:(c + 1) * P], ident[:])
            ins.then_inc(hT_done, 1)

        def first_transposes(q, index, t):
            pe.wait_ge(h_set, (2 * q[0] + q[1]) * TILES + t + 1)
            if not isinstance(index, int) or index >= 2:
                pe.wait_ge(hT_set, index - 1)
            transposes(index, xl[q[1]][:, t, :], t)

        def next_transposes(i, k, t):
            index = 2 * TILES + (4 * i + k) * TILES + t
            pe.wait_ge(affine_set, (4 * i + k) * TILES + t + 1)
            pe.wait_ge(hT_set, index - 1)
            transposes(index, act_rows[:, t % 2, :], t)

        def adj_transposes(q):
            i, g = q
            pe.wait_ge(adj_in[g], 48 * (i + 1))
            for t in range(TILES):
                ins = nc.tensor.transpose(psX[:, t * P:(t + 1) * P], adj_bd[g][:, t, :], ident[:])
            ins.then_inc(adjT_done, 1)

        def delta_transpose(i, k, t):
            n = (4 * i + k) * TILES + t
            pe.wait_ge(d_set, n + 1)
            if t >= 2:
                pe.wait_ge(dT_set, n - 1)
            nc.tensor.transpose(psX[:, (t % 2) * P:(t % 2 + 1) * P], delta[:, t % 2, :], ident[:]).then_inc(dT_done, 1)

        def product(i, k, j):
            if j >= 2:
                pe.wait_ge(m_set, (4 * i + k) * 2 * KC + j - 1)
            s, c = (LEFT, RIGHT)[j // KC], j % KC
            split_matmul(nc, psW[j % 2][:], w_cols(k // 2, s, slice(c * P, (c + 1) * P)), h_cols(k)).then_inc(m_done, 1)

        def bilinear(i, k, t):
            n = (4 * i + k) * TILES + t
            if t == 0:
                pe.wait_ge(m_set, (4 * i + k + 1) * 2 * KC)
            else:
                pe.wait_ge(u_set, n)
            for c in range(KC):
                for g in range(2):
                    nodes = slice(t * P + g * NODES, t * P + (g + 1) * NODES)
                    ins = nc.tensor.matmul(psU[NODES * g:NODES * (g + 1), 0:P].rearrange("p (s n) -> p s n", s=2),
                                           hT_whole[k % 2][:, c, nodes], m[:, :, c, nodes],
                                           start=(c == 0), stop=(c == KC - 1))
            ins.then_inc(u_done, 1)

        def linear(i, k, t):
            n = (4 * i + k) * TILES + t
            if t < 2:
                pe.wait_ge(m_set, (4 * i + k + 1) * 2 * KC - 1 + t)
            else:
                pe.wait_ge(lin_set, n - 1)
            split_matmul(nc, psW[t % 2][:, 0:D], h_cols(k, t), w_cols(k // 2, LIN, slice(0, D))).then_inc(lin_done, 1)

        def context(i, k, t):
            n = (4 * i + k) * TILES + t
            pe.wait_ge(dT_set, n + 1)
            pe.wait_ge(lin_set, n + 1)
            if t >= 2:
                pe.wait_ge(rows_set, n - 1)
            nc.tensor.matmul(psC[t % 2][:, 0:D + 1], dT[:, t % 2, :], lin[:, t % 2, :], start=True, stop=True)\
              .then_inc(c_done, 1)

        def products(i, k, tail):
            def left_T(t):
                if tail and tail[1] < 2:
                    next_transposes(*tail, t)

            if tail:
                pe.wait_ge(lin_set, (4 * tail[0] + tail[1] + 1) * TILES - 1)
            if tail and tail[1] in (0, 3):
                pe.wait_ge(dT_set, (4 * tail[0] + tail[1]) * TILES + 3)
                adj_transposes((tail[0], 1) if tail[1] == 0 else (i, 0))
            product(i, k, 0)
            if tail:
                if tail[1] in (0, 3):
                    pe.wait_ge(adjT_set, 2 * tail[0] + (2 if tail[1] == 0 else 3))
                delta_transpose(*tail, 3)
                left_T(0)
                pe.wait_ge(lin_set, (4 * tail[0] + tail[1] + 1) * TILES)
            product(i, k, 1)
            if tail:
                context(*tail, 3)
            product(i, k, 2)
            left_T(1)
            product(i, k, 3)
            left_T(2)
            product(i, k, 4)
            product(i, k, 5)
            left_T(3)
            if tail:
                pe.wait_ge(rows_set, (4 * tail[0] + tail[1] + 1) * TILES)

        def unit(i, k, ahead):
            for t in range(TILES):
                if t == 0:
                    linear(i, k, 0)
                if t == 3:
                    delta_transpose(i, k, 2)
                bilinear(i, k, t)
                if t in (1, 2):
                    delta_transpose(i, k, t - 1)
                if t < TILES - 1:
                    linear(i, k, t + 1)
                if k >= 2 and ahead:
                    first_transposes((i + 1, k - 2), 2 * TILES + (4 * i + k) * TILES + t, t)
                if t >= 1:
                    context(i, k, t - 1)
            if k < 3:
                if k == 1:
                    pe.wait_ge(w_lo_set, n_w)
                products(i, k + 1, (i, k))
            elif ahead:
                products(i + 1, 0, (i, 3))
            else:
                delta_transpose(i, k, 3)
                context(i, k, 3)

        for t in range(TILES):
            first_transposes((0, 0), t, t)
        adj_transposes((0, 0))
        pe.wait_ge(hT_set, TILES)
        for j in range(2 * KC):
            pe.wait_ge(w_lo_set, (LEFT, RIGHT)[j // KC] + 1)
            product(0, 0, j)
            if 1 <= j <= TILES:
                first_transposes((0, 1), TILES + j - 1, j - 1)
        pe.wait_ge(w_lo_set, LIN + 1)

        def turn(i, ahead):
            for k in range(4):
                unit(i, k, ahead)

        with pe.Fori(0, last) as i:
            turn(i, True)
        turn(last, False)


def directed_phase(nc, ctx, shared, x_in, adj, x_out, a, next_weights):
    w_hi, w_lo, raw, ident = shared["w_hi"], shared["w_lo"], shared["raw"], shared["ident"]
    n_w = 6
    temper = float(D) ** -0.5

    def sb(n, shape, dt=F32):
        return ctx.enter_context(nc.sbuf_tensor(f"l2_{n}", shape, dt))

    def ps(n):
        return ctx.enter_context(nc.psum_tensor(f"l2_{n}", [P, 512], F32))

    def sem(n):
        return ctx.enter_context(nc.semaphore(f"l2_{n}"))

    xl = [sb(f"xl{g}", [P, TILES, D]) for g in range(2)]
    xr = [sb(f"xr{g}", [P, TILES, D]) for g in range(2)]
    hT = [(sb(f"hT{k}_hi", [P, KC, COLS], F32R), sb(f"hT{k}_lo", [P, KC, COLS], F32R)) for k in range(4)]
    hT_whole = [sb(f"hT_whole{b}", [P, KC, COLS]) for b in range(2)]
    adj_rows = [sb(f"adj{g}", [P, TILES, NODES]) for g in range(2)]
    mx = sb("mx", [P, TILES])
    s_u = sb("s_u", [P, TILES, NODES])
    e_u = sb("e_u", [P, TILES, NODES])
    delta = sb("delta", [P, TILES, NODES])
    delta_diag = sb("delta_diag", [P, TILES, NODES])
    delta_sides = sb("delta_sides", [P, TILES, 2, NODES])
    z_sum, d_sum = sb("z_sum", [P, TILES]), sb("d_sum", [P, TILES])
    own = sb("own", [P, 2, TILES])
    r = sb("r", [P, 2, TILES])
    tri = sb("tri", [P, 2, NODES])
    eye = sb("eye", [P, NODES])
    dT = sb("dT", [P, TILES, P])
    sides = sb("sides", [P, 2, 2, D])
    selves = sb("selves", [P, 2, D])
    con = sb("con", [P, TILES, D])
    b_sides = sb("b_sides", [P, 2, D])
    b_s, ln_w, ln_b = (sb(n, [P, 2, D]) for n in ("b_s", "ln_w", "ln_b"))
    half = sb("half", [P, 1])
    stats = sb("stats", [P, TILES, 6])
    pause = sb("pause", [P, 1])
    mv = sb("mv", [P, TILES, 2])
    var = sb("var", [P, TILES])
    rstd = sb("rstd", [P, TILES])
    nbias = sb("nbias", [P, TILES])
    c_r2, c_var, c_root, c_scale, c_nb = (sb(n, [P, TILES]) for n in ("c_r2", "c_var", "c_root", "c_scale", "c_nb"))
    c_stats = sb("c_stats", [P, TILES, 6])
    c_mv = sb("c_mv", [P, TILES, 2])

    psU, psE, psC = ps("psU"), ps("psE"), ps("psC")
    psW = [ps(f"psW{b}") for b in range(3)]
    psT = [ps(f"psT{b}") for b in range(2)]

    w_hi_set = sem("w_hi_set")
    w_lo_set = sem("w_lo_set")
    zeroed = sem("zeroed")
    consts = sem("consts")
    xl_in = [sem(f"xl_in{g}") for g in range(2)]
    adj_in = [sem(f"adj_in{g}") for g in range(2)]
    xr_in = [sem(f"xr_in{g}") for g in range(2)]
    stored = [sem(f"stored{g}") for g in range(2)]
    var_set = sem("var_set")
    rstd_set = sem("rstd_set")
    nbias_set = sem("nbias_set")
    h_set = sem("h_set")
    hT_done = sem("hT_done")
    hT_hi_set = sem("hT_hi_set")
    hT_set = sem("hT_set")
    u_done = sem("u_done")
    s_set = sem("s_set")
    e_set = sem("e_set")
    delta_set = sem("delta_set")
    diag_set = sem("diag_set")
    parts_set = sem("parts_set")
    dT_done = sem("dT_done")
    dT_set = sem("dT_set")
    side_done = sem("side_done")
    side_set = sem("side_set")
    sides_set = sem("sides_set")
    self_done = sem("self_done")
    self_set = sem("self_set")
    c_done = sem("c_done")
    c_set = sem("c_set")
    c_var_set = sem("c_var_set")
    c_root_set = sem("c_root_set")
    c_ln_set = sem("c_ln_set")
    norm_set = sem("norm_set")
    affine_set = sem("affine_set")
    y_set = sem("y_set")
    dve_step = sem("dve_step")
    pool_step = sem("pool_step")

    def rows(ap, q):
        return ap[bass.ds(q * COLS, COLS), :].rearrange("(t p) n -> p t n", p=P)

    def T_index(i, k, t):
        return 2 * TILES + (4 * i + k) * TILES + t

    JOBS = {(0, 3): [(0, 0)],
            (1, 0): [(0, 1)], (1, 1): [(0, 2)], (1, 2): [(0, 3)], (1, 3): [(1, 0)],
            (2, 0): [(1, 1)], (2, 1): [(1, 2)], (2, 2): [(1, 3)], (2, 3): [(2, 0), (2, 1)],
            (3, 0): [(2, 2), (2, 3)], (3, 2): [(3, 0), (3, 1)], (3, 3): [(3, 2), (3, 3)]}

    def jobs(k, t, ahead):
        return [(source, x) for source, x in JOBS.get((k, t), []) if source < 2 or ahead]

    turns = GROUPS // 2
    last = turns - 1
    block = ctx.enter_context(nc.Block())

    @block.sync
    def _(sp):
        for g in range(2):
            sp.dma_start(xl[g][:], rows(x_in, g)).then_inc(xl_in[g], 16)
        for dst, name in ((b_s, "L2_gnn_bs"), (ln_w, "L2_gnn_ln_w"), (ln_b, "L2_gnn_ln_b")):
            sp.dma_start(dst[:], a[name].partition_broadcast(P)).then_inc(consts, 16)
        for s, name in enumerate(("L2_gnn_bl", "L2_gnn_br")):
            sp.dma_start(b_sides[NODES * s:NODES * (s + 1)], a[name].partition_broadcast(NODES)).then_inc(consts, 16)
        adj_flat = adj.rearrange("b q k -> (b q) k")
        for g in range(2):
            sp.dma_start(adj_rows[g][:], rows(adj_flat, g)).then_inc(adj_in[g], 16)
            sp.dma_start(xr[g][:], rows(x_in, g)).then_inc(xr_in[g], 16)
        sp.wait_ge(w_lo_set, n_w)
        load_weights(sp, raw, next_weights, shared["w_loaded"])

        def store(i, g, ahead):
            for t in range(TILES):
                sp.wait_ge(y_set, (2 * i + g) * TILES + t + 1)
                sp.dma_start(x_out[bass.ds((2 * i + g) * COLS + t * P, P), :], xr[g][:, t, :]).then_inc(stored[g], 16)
            sp.wait_ge(stored[g], (i + 1) * (16 * TILES))
            if ahead:
                sp.dma_start(xr[g][:], rows(x_in, 2 * i + 2 + g)).then_inc(xr_in[g], 16)

        def turn(i, ahead):
            if ahead:
                sp.wait_ge(hT_done, (4 * i + 2) * TILES)
                for g in range(2):
                    sp.dma_start(xl[g][:], rows(x_in, 2 * i + 2 + g)).then_inc(xl_in[g], 16)
                for g in range(2):
                    sp.wait_ge(delta_set, 4 * i + 3 + g)
                    sp.wait_ge(s_set, 4 * i + 3 + g)
                    sp.dma_start(adj_rows[g][:], rows(adj_flat, 2 * i + 2 + g)).then_inc(adj_in[g], 16)
            store(i, 0, ahead)
            store(i, 1, ahead)

        with sp.Fori(0, last) as i:
            turn(i, True)
        turn(last, False)

    @block.gpsimd
    def _(pool):
        step = Steps(pool, pool_step, 4 * TILES)
        pool.wait_ge(shared["ident_set"], 2)
        nc.gpsimd.memset(half[:], -0.5).then_inc(zeroed, 1)
        nc.gpsimd.memset(tri[:], 1.0).then_inc(zeroed, 1)
        nc.gpsimd.tensor_tensor(eye[:], ident[:, 0:NODES], ident[:, NODES:P], ALU.add).then_inc(zeroed, 1)
        pool.wait_ge(zeroed, 3)
        for s, sign in enumerate((1, -1)):
            for g in range(2):
                half_tri = tri[NODES * g:NODES * (g + 1), s, :]
                nc.gpsimd.affine_select(out=half_tri, in_=half_tri, compare_op=ALU.is_gt, fill=0.0, base=0,
                                        pattern=[[sign, NODES]], channel_multiplier=-sign).then_inc(zeroed, 1)
        pool.wait_ge(zeroed, 7)

        def roots(q):
            pool.wait_ge(var_set, q + 1)
            nc.gpsimd.tensor_tensor(rstd[:], var[:], half[:].broadcast_to([P, TILES]), ALU.pow).then_inc(rstd_set, 1)

        def diagonal(i, k):
            pool.wait_ge(delta_set, 4 * i + k + 1)
            nc.gpsimd.tensor_tensor(delta_diag[:], delta[:], eye[:].rearrange("p (t n) -> p t n", t=1)
                                    .broadcast_to([P, TILES, NODES]), ALU.mult).then_inc(diag_set, 1)

        def side_biases(i, k, t):
            n = (4 * i + k) * TILES + t
            pool.wait_ge(side_set, 2 * n + 2)
            nc.gpsimd.tensor_tensor(sides[:, t % 2], sides[:, t % 2],
                                    b_sides[:, k // 2, :].rearrange("p (g n) -> p g n", g=1).broadcast_to([P, 2, D]),
                                    ALU.add).then_inc(sides_set, 1)

        def root(i, k, t):
            pool.wait_ge(c_var_set, (4 * i + k) * TILES + t + 1)
            nc.gpsimd.tensor_tensor(c_root[:, t:t + 1], c_var[:, t:t + 1], half[:], ALU.pow).then_inc(c_root_set, 1)

        def affine(i, k, t):
            pool.wait_ge(norm_set, (4 * i + k) * TILES + t + 1)
            step.done(nc.gpsimd.tensor_tensor(con[:, t, :], con[:, t, :], ln_w[:, k // 2, :], ALU.mult))
            nc.gpsimd.tensor_tensor(con[:, t, :], con[:, t, :], ln_b[:, k // 2, :], ALU.add).then_inc(affine_set, 1)

        roots(0)
        roots(1)
        pool.wait_ge(consts, 80)
        diagonal(0, 0)
        side_biases(0, 0, 0)

        def turn(i, ahead):
            step.turn(i, 0)
            for k in range(4):
                following = (i, k + 1) if k < 3 else (i + 1, 0)
                for t in range(1, TILES):
                    side_biases(i, k, t)
                    if t == 3:
                        affine(i, k, 1)
                        if k < 3 or ahead:
                            diagonal(*following)
                    root(i, k, t - 1)
                    if t == 2:
                        affine(i, k, 0)
                if k < 3 or ahead:
                    side_biases(*following, 0)
                if ahead and k in (1, 2):
                    roots(2 * i + k + 1)
                affine(i, k, 2)
                root(i, k, 3)
                affine(i, k, 3)

        with pool.Fori(0, last) as i:
            turn(i, True)
            step.ended()
        turn(last, False)

    @block.scalar
    def _(act):
        act.wait_ge(shared["w_loaded"], shared["w_count"]["l2"])

        def weights(slots):
            for s in slots:
                nc.scalar.activation(w_hi[:, s], raw[:, s], ACT.Copy).then_inc(w_hi_set, 1)


        def normalise(q, tiles=range(TILES)):
            act.wait_ge(nbias_set, 2 * q[0] + q[1] + 1)
            for t in tiles:
                nc.scalar.activation(xl[q[1]][:, t, :], xl[q[1]][:, t, :], ACT.Relu, bias=nbias[:, t:t + 1],
                                     scale=rstd[:, t:t + 1]).then_inc(h_set, 1)

        def hT_part(index, unit, t):
            act.wait_ge(hT_done, index + 1)
            nc.scalar.activation(hT_whole[unit == 1][:, :, t * P:(t + 1) * P],
                                 psT[t % 2][:, 0:D].rearrange("p (c n) -> p c n", c=KC), ACT.Relu)
            nc.scalar.activation(hT[unit][0][:, :, t * P:(t + 1) * P],
                                 psT[t % 2][:, 0:D].rearrange("p (c n) -> p c n", c=KC), ACT.Relu).then_inc(hT_hi_set, 1)

        def exponential(i, k):
            act.wait_ge(s_set, 4 * i + k + 1)
            nc.scalar.activation(e_u[:], s_u[:], ACT.Exp, scale=temper).then_inc(e_set, 1)

        def attention_parts(i, k):
            act.wait_ge(dT_done, 4 * i + k + 1)
            nc.scalar.activation(dT[:].rearrange("p t n -> p (t n)"), psE[:], ACT.Copy).then_inc(dT_set, 1)

        def norm_rows(i, k, t):
            act.wait_ge(c_ln_set, (4 * i + k) * TILES + t + 1)
            nc.scalar.activation(con[:, t, :], con[:, t, :], ACT.Identity, bias=c_nb[:, t:t + 1],
                                 scale=c_scale[:, t:t + 1]).then_inc(norm_set, 1)

        def side_copies(i, k, t):
            n = (4 * i + k) * TILES + t
            if not (isinstance(i, int) and i == 0 and k == 0 and t < 2):
                act.wait_ge(c_done, n - 1)
            for s in range(2):
                act.wait_ge(side_done, 2 * n + s + 1)
                for g in range(2):
                    ins = nc.scalar.activation(sides[NODES * s:NODES * (s + 1), t % 2, g, :],
                                               psW[s][NODES * g:NODES * (g + 1), 0:D], ACT.Copy)
                ins.then_inc(side_set, 1)

        def slot(i, k, t, ahead):
            if t >= 2:
                norm_rows(i, k, t - 2)
            side_copies(i, k, t)
            if ahead and t in (1, 2) and k >= 2:
                normalise((i + 1, k - 2), (2 * t - 2, 2 * t - 1))
            following = (i, k + 1) if k < 3 else (i + 1, 0)
            more = k < 3 or ahead
            if t == 3 and more:
                exponential(*following)
            for source, x in jobs(k, t, ahead):
                hT_part(T_index(i, source, x), (source + 2) % 4, x)
            if t == 3:
                if more:
                    side_copies(*following, 0)
                norm_rows(i, k, 2)
                if more:
                    attention_parts(*following)
                    for source, x in jobs(k + 1, 0, ahead):
                        hT_part(T_index(i, source, x), (source + 2) % 4, x)
                norm_rows(i, k, 3)

        weights((0, 1, 2))
        normalise((0, 0))
        for t in range(TILES):
            hT_part(t, 0, t)
        normalise((0, 1))
        exponential(0, 0)
        side_copies(0, 0, 0)
        hT_part(TILES, 1, 0)
        hT_part(TILES + 1, 1, 1)
        attention_parts(0, 0)
        hT_part(TILES + 2, 1, 2)
        hT_part(TILES + 3, 1, 3)
        weights((3, 4, 5))

        def turn(i, ahead):
            for k in range(4):
                for t in range(1, TILES):
                    slot(i, k, t, ahead)

        with act.Fori(0, last) as i:
            turn(i, True)
        turn(last, False)

    @block.vector
    def _(dve):
        step = Steps(dve, dve_step, 0)

        def weights(slots):
            for s in slots:
                dve.wait_ge(w_hi_set, s + 1)
                nc.vector.tensor_tensor(w_lo[:, s], raw[:, s], w_hi[:, s].bitcast(F32), ALU.subtract)\
                  .then_inc(w_lo_set, 1)


        def statistics(q, tiles=range(TILES)):
            if tiles[0] == 0:
                dve.wait_ge(xl_in[q[1]], q[0] * 16 + 16)
            for t in tiles:
                ins = nc.vector.bn_stats(stats[:, t, :], xl[q[1]][:, t, :])
            if tiles[-1] == TILES - 1:
                step.mark(ins)

        def variances():
            step.catch_up()
            nc.vector.memset(pause[:], 0.0)
            for t in range(TILES):
                ins = nc.vector.bn_aggr(mv[:, t, :], stats[:, t, :])
            step.done(ins)
            nc.vector.tensor_scalar(var[:], mv[:, :, 1], LN_EPS, None, ALU.add).then_inc(var_set, 1)

        def shifts(q):
            dve.wait_ge(rstd_set, 2 * q[0] + q[1] + 1)
            nc.vector.scalar_tensor_tensor(nbias[:], mv[:, :, 0], -1.0, rstd[:], ALU.mult, ALU.mult)\
              .then_inc(nbias_set, 1)

        def hT_part(index, unit, t):
            dve.wait_ge(hT_hi_set, index + 1)
            hi, lo = (x[:, :, t * P:(t + 1) * P] for x in hT[unit])
            nc.vector.scalar_tensor_tensor(lo, psT[t % 2][:, 0:D].rearrange("p (c n) -> p c n", c=KC), 0.0,
                                           hi.bitcast(F32), ALU.max, ALU.subtract).then_inc(hT_set, 1)

        def less_maximum(i, k):
            dve.wait_ge(u_done, 4 * i + k + 1)
            u = psU[:, 0:TILES * NODES].rearrange("p (t n) -> p t n", t=TILES)
            step.done(nc.vector.tensor_reduce(mx[:], u, axis=AX.X, op=ALU.max))
            most = mx[:].rearrange("p (t n) -> p t n", n=1).broadcast_to([P, TILES, NODES])
            nc.vector.tensor_tensor(s_u[:], u, most, ALU.subtract).then_inc(s_set, 1)

        def attention_sides(i, k):
            dve.wait_ge(e_set, 4 * i + k + 1)
            dve.wait_ge(adj_in[k % 2], (i + 1) * 16)
            nc.vector.tensor_tensor(delta[:], e_u[:], adj_rows[k % 2][:], ALU.mult).then_inc(delta_set, 1)
            dve.wait_ge(delta_set, 4 * i + k + 1)
            whole = delta[:].rearrange("p t (s n) -> p t s n", s=1).broadcast_to([P, TILES, 2, NODES])
            side = tri[:].rearrange("p (t s) n -> p t s n", t=1).broadcast_to([P, TILES, 2, NODES])
            nc.vector.tensor_tensor(delta_sides[:], whole, side, ALU.mult).then_inc(parts_set, 1)

        def row_factors(i, k):
            step.mark(nc.vector.tensor_reduce(z_sum[:], e_u[:], axis=AX.X, op=ALU.add))
            step.done(nc.vector.tensor_reduce(d_sum[:], delta[:], axis=AX.X, op=ALU.add))
            step.done(nc.vector.scalar_tensor_tensor(r[:, k % 2, :], z_sum[:], 1e-10, d_sum[:], ALU.mult, ALU.add))
            step.mark(nc.vector.reciprocal(r[:, k % 2, :], r[:, k % 2, :]))
            dve.wait_ge(diag_set, 4 * i + k + 1)
            step.done(nc.vector.tensor_reduce(own[:, k % 2, :], delta_diag[:], axis=AX.X, op=ALU.add))

        def self_copy(i, k, t):
            dve.wait_ge(self_done, (4 * i + k) * TILES + t + 1)
            nc.vector.tensor_tensor(selves[:, t % 2, :], psW[2][:, 0:D], b_s[:, k // 2, :], ALU.add).then_inc(self_set, 1)

        def context(i, k, t):
            n = (4 * i + k) * TILES + t
            one = slice(t, t + 1)
            dve.wait_ge(c_done, n + 1)
            dve.wait_ge(self_set, n + 1)
            nc.vector.scalar_tensor_tensor(con[:, t, :], selves[:, t % 2, :], own[:, k % 2, one], psC[:, 0:D],
                                           ALU.mult, ALU.add).then_inc(c_set, 1)

        def context_variance(i, k, t):
            n = (4 * i + k) * TILES + t
            one = slice(t, t + 1)
            dve.wait_ge(c_set, n + 1)
            step.done(nc.vector.bn_stats(c_stats[:, t, :], con[:, t, :]))
            nc.vector.tensor_tensor(c_r2[:, one], r[:, k % 2, one], r[:, k % 2, one], ALU.mult)
            step.done(nc.vector.bn_aggr(c_mv[:, t, :], c_stats[:, t, :]))
            nc.vector.tensor_scalar(c_var[:, one], c_mv[:, t, 1:2], c_r2[:, one], 1e-12, ALU.mult, ALU.add)\
              .then_inc(c_var_set, 1)

        def context_norm(i, k, t):
            one = slice(t, t + 1)
            dve.wait_ge(c_root_set, (4 * i + k) * TILES + t + 1)
            step.done(nc.vector.tensor_tensor(c_scale[:, one], c_root[:, one], r[:, k % 2, one], ALU.mult))
            nc.vector.scalar_tensor_tensor(c_nb[:, one], c_mv[:, t, 0:1], -1.0, c_scale[:, one], ALU.mult, ALU.mult)\
              .then_inc(c_ln_set, 1)

        def result(i, k, t):
            g = k - 2
            if t == 0:
                dve.wait_ge(xr_in[g], (i + 1) * 16)
            dve.wait_ge(affine_set, (4 * i + k) * TILES + t + 1)
            nc.vector.scalar_tensor_tensor(xr[g][:, t, :], con[:, t, :], 0.0, xr[g][:, t, :], ALU.max, ALU.add)\
              .then_inc(y_set, 1)

        def slot(i, k, t, ahead):
            following = (i, k + 1) if k < 3 else (i + 1, 0)
            more = k < 3 or ahead
            if t >= 2:
                context_norm(i, k, t - 2)
            if ahead and t == 1 and k >= 2:
                shifts((i + 1, k - 2))
            self_copy(i, k, t)
            if t == 3 and more:
                less_maximum(*following)
            context(i, k, t - 1)
            if t == 3 and more:
                attention_sides(*following)
            context_variance(i, k, t - 1)
            for source, x in jobs(k, t, ahead):
                hT_part(T_index(i, source, x), (source + 2) % 4, x)
            if k == 3 and t < 3:
                result(i, 2, t + 1)
            if k >= 2 and t == 3:
                result(i, k, 0)
            if ahead and t < 3 and k in (1, 2):
                statistics((i + 1, k - 1), (2 * t - 2, 2 * t - 1))
            if t == 3:
                if more:
                    row_factors(*following)
                if ahead and k in (1, 2):
                    variances()
                context_norm(i, k, 2)
                context(i, k, 3)
                if more:
                    self_copy(*following, 0)
                context_variance(i, k, 3)
                if more:
                    for source, x in jobs(k + 1, 0, ahead):
                        hT_part(T_index(i, source, x), (source + 2) % 4, x)
                if k == 2:
                    result(i, 2, 1)
                context_norm(i, k, 3)
                if k == 3:
                    for x in range(1, TILES):
                        result(i, 3, x)

        statistics((0, 0))
        variances()
        weights((0,))
        shifts((0, 0))
        statistics((0, 1))
        for t in range(TILES):
            hT_part(t, 0, t)
        variances()
        dve.wait_ge(consts, 80)
        dve.wait_ge(zeroed, 7)
        shifts((0, 1))
        weights((1,))
        less_maximum(0, 0)
        weights((2,))
        attention_sides(0, 0)
        row_factors(0, 0)
        hT_part(TILES, 1, 0)
        hT_part(TILES + 1, 1, 1)
        self_copy(0, 0, 0)
        hT_part(TILES + 2, 1, 2)
        hT_part(TILES + 3, 1, 3)
        weights((3, 4, 5))
        before = step.n
        step.per = 4 * (1 + 5 + TILES * (2 + 1)) + 2 * 2

        def turn(i, ahead):
            step.turn(i, before)
            for k in range(4):
                for t in range(1, TILES):
                    slot(i, k, t, ahead)

        with dve.Fori(0, last) as i:
            turn(i, True)
            step.ended()
        turn(last, False)

    @block.tensor
    def _(pe):
        pe.wait_ge(shared["ident_set"], 2)
        LEFT, RIGHT, SELF = range(3)

        def h_cols(k, t):
            return tuple((lambda c, x=x: x[:, c, t * P:(t + 1) * P]) for x in hT[k])

        def projection(k, s):
            return tuple((lambda c, w=w: w[:, 3 * (k // 2) + s, c, :]) for w in (w_hi, w_lo))

        def transposes(index, src, t):
            if not (isinstance(index, int) and index < 2):
                pe.wait_ge(hT_set, index - 1)
            for c in range(KC):
                ins = nc.tensor.transpose(psT[t % 2][:, c * P:(c + 1) * P], src[:, c * P:(c + 1) * P], ident[:])
            ins.then_inc(hT_done, 1)

        def products(i, k):
            pe.wait_ge(hT_set, (4 * i + (1, 2, 3, 4)[k]) * TILES)
            if not (isinstance(i, int) and i == 0 and k == 0):
                pe.wait_ge(s_set, 4 * i + k)
            for t in range(TILES):
                for c in range(KC):
                    for g in range(2):
                        lo = t * P + g * NODES
                        nodes = hT_whole[k == 1][:, c, lo:lo + NODES]
                        ins = nc.tensor.matmul(psU[NODES * g:NODES * (g + 1), t * NODES:(t + 1) * NODES], nodes, nodes,
                                               start=(c == 0), stop=(c == KC - 1))
            ins.then_inc(u_done, 1)

        def delta_transposes(i, k):
            pe.wait_ge(parts_set, 4 * i + k + 1)
            for t in range(TILES):
                ins = nc.tensor.transpose(psE[:, t * P:(t + 1) * P], delta_sides[:, t].rearrange("p s n -> p (s n)"),
                                          ident[:])
            ins.then_inc(dT_done, 1)

        def side(i, k, t, s):
            n = (4 * i + k) * TILES + t
            if not (isinstance(i, int) and i == 0 and k == 0 and t == 0):
                pe.wait_ge(side_set, 2 * n - 1 + s)
            split_matmul(nc, psW[s][:, 0:D], h_cols(k, t), projection(k, s)).then_inc(side_done, 1)

        def self_part(i, k, t):
            n = (4 * i + k) * TILES + t
            if t >= 1:
                pe.wait_ge(self_set, n)
            split_matmul(nc, psW[2][:, 0:D], h_cols(k, t), projection(k, SELF)).then_inc(self_done, 1)

        def context(i, k, t):
            n = (4 * i + k) * TILES + t
            if t == 0:
                pe.wait_ge(dT_set, 4 * i + k + 1)
            else:
                pe.wait_ge(c_set, n)
            pe.wait_ge(sides_set, n + 1)
            for g in range(2):
                graph = slice(NODES * g, NODES * (g + 1))
                ins = nc.tensor.matmul(psC[graph, 0:D], dT[:, t, graph], sides[:, t % 2, g, :], start=True, stop=True)
            ins.then_inc(c_done, 1)

        def transpose_jobs(i, k, t, ahead):
            for source, x in jobs(k, t, ahead):
                if source < 2:
                    pe.wait_ge(affine_set, (4 * i + source) * TILES + x + 1)
                    transposes(T_index(i, source, x), con[:, x, :], x)
                else:
                    pe.wait_ge(h_set, (2 * i + source) * TILES + x + 1)
                    transposes(T_index(i, source, x), xl[source - 2][:, x, :], x)

        def slot(i, k, t, ahead):
            following = (i, k + 1) if k < 3 else (i + 1, 0)
            more = k < 3 or ahead
            side(i, k, t, 0)
            side(i, k, t, 1)
            self_part(i, k, t)
            if t == 3 and more:
                products(*following)
            context(i, k, t - 1)
            transpose_jobs(i, k, t, ahead)
            if t == 3:
                if k == 1:
                    pe.wait_ge(w_lo_set, n_w)
                if more:
                    side(*following, 0, 0)
                    side(*following, 0, 1)
                context(i, k, 3)
                if more:
                    delta_transposes(*following)
                    pe.wait_ge(self_set, (4 * i + k + 1) * TILES)
                    self_part(*following, 0)
                    transpose_jobs(i, k + 1, 0, ahead)

        def first_transposes(q, tiles):
            for t in tiles:
                pe.wait_ge(h_set, q * TILES + t + 1)
                transposes(q * TILES + t, xl[q][:, t, :], t)

        first_transposes(0, range(TILES))
        products(0, 0)
        for s in range(2):
            pe.wait_ge(w_lo_set, s + 1)
            side(0, 0, 0, s)
        first_transposes(1, (0, 1))
        delta_transposes(0, 0)
        pe.wait_ge(w_lo_set, SELF + 1)
        self_part(0, 0, 0)
        first_transposes(1, (2, 3))

        def turn(i, ahead):
            for k in range(4):
                for t in range(1, TILES):
                    slot(i, k, t, ahead)

        with pe.Fori(0, last) as i:
            turn(i, True)
        turn(last, False)


PHASE_WEIGHTS = {
    "l0": ["L0_gnn_Wq", "L0_gnn_Wk", "L0_gnn_Wv", "L0_gnn_Wo"],
    "l1": ["L1_gnn_W_left0", "L1_gnn_W_right0", "L1_gnn_W_lin0", "L1_gnn_W_left1", "L1_gnn_W_right1", "L1_gnn_W_lin1"],
    "l2": ["L2_gnn_Wl0", "L2_gnn_Wr0", "L2_gnn_Ws0", "L2_gnn_Wl1", "L2_gnn_Wr1", "L2_gnn_Ws1"],
    "l3": ["L3_gnn_Wq", "L3_gnn_Wk", "L3_gnn_Wv"],
}
PHASES = ["l0", "l1", "l2", "l3"]


def build(nc, a, out, phases=PHASES):
    x = a["x"].rearrange("b n d -> (b n) d")
    adj_rows = a["adj"].rearrange("b q k -> (b q) k")
    out_rows = out.rearrange("b n d -> (b n) d")
    graph_phase = {"l1": bilinear_phase, "l2": directed_phase}
    with ExitStack() as ctx:
        shared = {
            "w_hi": ctx.enter_context(nc.sbuf_tensor("w_hi", [P, SLOTS, KC, D], F32R)),
            "w_lo": ctx.enter_context(nc.sbuf_tensor("w_lo", [P, SLOTS, KC, D], F32R)),
            "raw": ctx.enter_context(nc.sbuf_tensor("w_raw", [P, SLOTS, KC, D], F32)),
            "ident": ctx.enter_context(nc.sbuf_tensor("ident", [P, P], F32)),
            "w_loaded": ctx.enter_context(nc.semaphore("w_loaded")),
            "ident_set": ctx.enter_context(nc.semaphore("ident_set")),
            "w_count": {},
        }
        n = 0
        for name in phases:
            n += 16 * len(PHASE_WEIGHTS[name])
            shared["w_count"][name] = n
        weights = {name: [a[w] for w in PHASE_WEIGHTS[name]] for name in phases}

        with nc.Block() as block:
            if not phases[0] in ("l0", "l3"):
                @block.sync
                def _(sp):
                    load_weights(sp, shared["raw"], weights[phases[0]], shared["w_loaded"])

            @block.gpsimd
            def _(pool):
                ident = shared["ident"]
                nc.gpsimd.memset(ident[:], 0.0).then_inc(shared["ident_set"], 1)
                pool.wait_ge(shared["ident_set"], 1)
                nc.gpsimd.affine_select(out=ident[:], in_=ident[:], compare_op=ALU.not_equal, fill=1.0, base=0,
                                        pattern=[[-1, P]], channel_multiplier=1).then_inc(shared["ident_set"], 1)

        def across(v):
            return v.partition_broadcast(P)

        source = x
        for k, name in enumerate(phases):
            last = k == len(phases) - 1
            target = out_rows if last else nc.dram_tensor(f"after_{name}", (ROWS, D), F32, kind="Internal").ap()
            own = weights[name] if k == 0 else []
            following = [] if last else weights[phases[k + 1]]
            with ExitStack() as phase:
                if name == "l0":
                    def biases(bv, bo, b_q, b_k, beta):
                        return [(bv[:], across(a["L0_gnn_bv"])), (bo[:], across(a["L0_gnn_bo"]))]
                    attention_phase(nc, phase, name, shared, source, adj_rows, target, biases, own, following)
                elif name == "l3":
                    def biases(bv, bo, b_q, b_k, beta):
                        return [(bv[:], across(a["L3_gnn_bv"])), (b_q[:], a["L3_gnn_bq"]), (b_k[:], a["L3_gnn_bk"]),
                                (beta[:], a["L3_gnn_beta"].partition_broadcast(P))]
                    attention_phase(nc, phase, name, shared, source, adj_rows, target, biases, own, following)
                else:
                    graph_phase[name](nc, phase, shared, source, a["adj"], target, a, following)
            source = target


def laid_out(inputs):
    import numpy as np

    arrays = {}
    for n, v in inputs.items():
        v = np.ascontiguousarray(v)
        if n == "L3_gnn_beta":
            arrays[n] = v.reshape(1)
        elif n in ("L3_gnn_bq", "L3_gnn_bk"):
            arrays[n] = np.ascontiguousarray(v.reshape(KC, P).T)
        elif n in ("L0_gnn_Wq", "L0_gnn_Wk", "L0_gnn_Wv", "L0_gnn_Wo"):
            arrays[n] = np.ascontiguousarray(v.T)
        elif n in ("L1_gnn_W_left", "L1_gnn_W_right", "L1_gnn_W_lin", "L2_gnn_Wl", "L2_gnn_Wr", "L2_gnn_Ws"):
            for layer in range(2):
                arrays[f"{n}{layer}"] = np.ascontiguousarray(v[layer].T)
        else:
            arrays[n] = v
    return arrays


def kernel(**inputs):
    import concourse.bacc as bacc
    from concourse.bass_utils import run_bass_kernel_spmd

    arrays = laid_out(inputs)
    nc = bacc.Bacc("TRN2", target_bir_lowering=False, num_devices=1)
    a = {n: nc.dram_tensor(f"in_{n}", v.shape, mybir.dt.from_np(v.dtype), kind="ExternalInput").ap()
         for n, v in arrays.items()}
    out = nc.dram_tensor("out_x", (GRAPHS, NODES, D), F32, kind="ExternalOutput").ap()
    build(nc, a, out)
    r = run_bass_kernel_spmd(nc, [{f"in_{n}": v for n, v in arrays.items()}], core_ids=[0])
    return r.results[0]["out_x"]
```
